# Optimizing a Trainium2 kernel written in Bass

```python
import numpy as np
import jax
import jax.numpy as jnp

def _softmax(x, axis=-1):
    return jax.nn.softmax(x, axis=axis)

def _gelu(x):
    return jax.nn.gelu(x, approximate=True)

def _silu(x):
    return jax.nn.silu(x)

def _sigmoid(x):
    return jax.nn.sigmoid(x)

def _layernorm(x, axis=-1, eps=1e-05):
    m = jnp.mean(x, axis=axis, keepdims=True)
    v = jnp.var(x, axis=axis, keepdims=True)
    return (x - m) / jnp.sqrt(v + eps)

def _scatter_add(tgt, idx, src, axis=0):
    return tgt.at[idx].add(src)

def _segment_sum(src, seg, n):
    return jax.ops.segment_sum(src, seg, n)
kernel_name = 'mk_decoder_preln_d1_seqx_r4_c040ac'

def setup_inputs(seed: int=0):
    np.random.seed(seed)
    _w = jnp.asarray

    def _rec_inputs():
        import jax
        import jax.numpy as jnp
        _rk = jax.random.key(seed)
        x = -0.0002928 + 1 * jax.random.normal(jax.random.fold_in(_rk, 1), (4, 512, 256), jnp.float32)
        _lenS = 512 - jax.random.randint(jax.random.fold_in(_rk, 7), (4,), 0, max(1, 512 // 4) + 1, jnp.int32)
        _lenS2 = 512 - jax.random.randint(jax.random.fold_in(_rk, 8), (4,), 0, max(1, 512 // 4) + 1, jnp.int32)
        _ctx_1024P = jax.random.normal(jax.random.fold_in(_rk, 11), (4, 16, 256), jnp.float32)
        _ctx_1024c = jax.random.dirichlet(jax.random.fold_in(_rk, 511), 0.3 * jnp.ones((16,), jnp.float32), (4, 512))
        _ctx_1024t = jnp.einsum('bsk,bkd->bsd', _ctx_1024c, _ctx_1024P)
        _ctx_1024t = _ctx_1024t * jax.lax.rsqrt(jnp.mean(jnp.square(_ctx_1024t)) + 1e-12) * 0.953939
        ctx_1024 = 4.13588e-05 + 0.999923 * (_ctx_1024t + 0.3 * jax.random.normal(jax.random.fold_in(_rk, 611), (4, 512, 256), jnp.float32))
        return (x, ctx_1024)
    x, ctx_1024 = _rec_inputs()

    def _L0_attn_setup():
        import math
        import jax, jax.numpy as jnp
        import numpy as np
        from jax import lax
        D_MODEL = 256
        N_LAYERS = 2
        D_STATE = 16
        D_CONV = 4
        EXPAND = 2
        D_INNER = EXPAND * D_MODEL
        DT_RANK = math.ceil(D_MODEL / 16)
        BATCH = 2
        SEQLEN = 256
        BETA = 0.6
        ALPHA = 1.0
        EPS = 1e-05
        DT_MIN, DT_MAX, DT_FLOOR = (0.001, 0.1, 0.0001)

        def _rmsnorm(x, w):
            return x * jax.lax.rsqrt(jnp.mean(x * x, axis=-1, keepdims=True) + EPS) * w

        def _block(x, in_w, cw, cb, xp_w, dtw, dtb, a_log, dp, ow):
            B, L, _ = x.shape
            xz = jnp.einsum('bld,ed->ble', x, in_w)
            xb, z = jnp.split(xz, 2, axis=-1)
            xc = lax.conv_general_dilated(xb.transpose(0, 2, 1), cw[:, None, :], window_strides=(1,), padding=[(D_CONV - 1, 0)], dimension_numbers=('NCH', 'OIH', 'NCH'), feature_group_count=D_INNER)
            xb = jax.nn.silu((xc + cb[None, :, None]).transpose(0, 2, 1))
            dbc = jnp.einsum('ble,re->blr', xb, xp_w)
            delta = dbc[..., :DT_RANK]
            Bm = dbc[..., DT_RANK:DT_RANK + D_STATE]
            Cm = dbc[..., DT_RANK + D_STATE:]
            delta = jax.nn.softplus(jnp.einsum('blr,er->ble', delta, dtw) + dtb)
            dA = jnp.exp(delta[..., None] * -jnp.exp(a_log))
            mi = ALPHA * delta[..., None] * Bm[:, :, None, :] * xb[..., None]

            def scan_fn(carry, inp):
                h, v = carry
                dA_t, mi_t, C_t = inp
                v = BETA * v + mi_t
                h = dA_t * h + v
                y_t = jnp.einsum('ben,bn->be', h, C_t)
                return ((h, v), y_t)
            h0 = jnp.zeros((B, D_INNER, D_STATE), dtype=x.dtype)
            _, ys = lax.scan(scan_fn, (h0, h0), (dA.transpose(1, 0, 2, 3), mi.transpose(1, 0, 2, 3), Cm.transpose(1, 0, 2)))
            y = ys.transpose(1, 0, 2) + dp * xb
            y = y * jax.nn.silu(z)
            return jnp.einsum('ble,de->bld', y, ow)
        key = jax.random.key(seed)
        ks = jax.random.split(key, 10)
        std = 0.02
        nl = N_LAYERS
        x = jax.random.normal(ks[0], (BATCH, SEQLEN, D_MODEL), dtype=jnp.float32)
        in_proj_w = jax.random.normal(ks[1], (nl, 2 * D_INNER, D_MODEL), dtype=jnp.float32) * std
        conv_w = jax.random.normal(ks[2], (nl, D_INNER, D_CONV), dtype=jnp.float32) * std
        conv_b = jnp.zeros((nl, D_INNER), dtype=jnp.float32)
        x_proj_w = jax.random.normal(ks[3], (nl, DT_RANK + 2 * D_STATE, D_INNER), dtype=jnp.float32) * std
        dt_std = DT_RANK ** (-0.5)
        dt_w = jax.random.uniform(ks[4], (nl, D_INNER, DT_RANK), dtype=jnp.float32, minval=-dt_std, maxval=dt_std)
        dt = jnp.exp(jax.random.uniform(ks[5], (nl, D_INNER), dtype=jnp.float32) * (math.log(DT_MAX) - math.log(DT_MIN)) + math.log(DT_MIN))
        dt = jnp.clip(dt, DT_FLOOR, None)
        dt_b = dt + jnp.log(-jnp.expm1(-dt))
        A_log = jnp.broadcast_to(jnp.log(jnp.arange(1, D_STATE + 1, dtype=jnp.float32)), (nl, D_INNER, D_STATE)).copy()
        Dp = jnp.ones((nl, D_INNER), dtype=jnp.float32)
        out_w = jax.random.normal(ks[6], (nl, D_MODEL, D_INNER), dtype=jnp.float32) * std
        norm_w = jnp.ones((nl, D_MODEL), dtype=jnp.float32)
        return {'x': x, 'norm_w': norm_w, 'in_proj_w': in_proj_w, 'conv_w': conv_w, 'conv_b': conv_b, 'x_proj_w': x_proj_w, 'dt_w': dt_w, 'dt_b': dt_b, 'A_log': A_log, 'Dp': Dp, 'out_w': out_w}
    _L0_attn_all = _L0_attn_setup()
    _L0_attn_in = {k: v for k, v in _L0_attn_all.items() if k in ('norm_w', 'in_proj_w', 'conv_w', 'conv_b', 'x_proj_w', 'dt_w', 'dt_b', 'A_log', 'Dp', 'out_w')}
    del _L0_attn_all

    def _L0_xattn_setup():
        import jax, jax.numpy as jnp
        import numpy as np
        HIDDEN = 256
        NUM_HEADS = 16
        HEAD_DIM = HIDDEN // NUM_HEADS
        SCALE = 1.0 / float(np.sqrt(HEAD_DIM))
        key = jax.random.key(seed)
        ks = jax.random.split(key, 10)
        B, SQ, SKV = (2, 512, 1024)
        init = 0.02
        return {'query_states': jax.random.normal(ks[0], (B, SQ, HIDDEN), dtype=jnp.float32), 'key_value_states': jax.random.normal(ks[1], (B, SKV, HIDDEN), dtype=jnp.float32), 'Wq': jax.random.normal(ks[2], (HIDDEN, HIDDEN), dtype=jnp.float32) * init, 'bq': jnp.zeros((HIDDEN,), dtype=jnp.float32), 'Wk': jax.random.normal(ks[3], (HIDDEN, HIDDEN), dtype=jnp.float32) * init, 'bk': jnp.zeros((HIDDEN,), dtype=jnp.float32), 'Wv': jax.random.normal(ks[4], (HIDDEN, HIDDEN), dtype=jnp.float32) * init, 'bv': jnp.zeros((HIDDEN,), dtype=jnp.float32), 'Wo': jax.random.normal(ks[5], (HIDDEN, HIDDEN), dtype=jnp.float32) * init, 'bo': jnp.zeros((HIDDEN,), dtype=jnp.float32)}
    _L0_xattn_all = _L0_xattn_setup()
    _L0_xattn_in = {k: v for k, v in _L0_xattn_all.items() if k in ('Wq', 'bq', 'Wk', 'bk', 'Wv', 'bv', 'Wo', 'bo')}
    del _L0_xattn_all

    def _L0_ffn_setup():
        import jax, jax.numpy as jnp
        import numpy as np
        TOP_K = 2

        def _gelu(x):
            return jax.nn.gelu(x, approximate=False)
        key = jax.random.key(seed)
        ks = jax.random.split(key, 6)
        B, S, D, F, E = (2, 512, 256, 512, 8)
        sc_g = 1.0 / np.sqrt(D)

        def xav(k, shape, fan_in, fan_out):
            lim = np.sqrt(6.0 / (fan_in + fan_out))
            return jax.random.uniform(k, shape, jnp.float32, -lim, lim)
        return {'x': jax.random.normal(ks[0], (B, S, D), jnp.float32), 'Wg': xav(ks[1], (D, E), D, E), 'Wu': xav(ks[2], (E, D, F), D, F), 'Wd': xav(ks[3], (E, F, D), F, D), 'W1': xav(ks[4], (D, F), D, F), 'W2': xav(ks[5], (F, D), F, D)}
    _L0_ffn_all = _L0_ffn_setup()
    _L0_ffn_in = {k: v for k, v in _L0_ffn_all.items() if k in ('Wg', 'Wu', 'Wd', 'W1', 'W2')}
    del _L0_ffn_all
    return {'x': x, 'ctx_1024': ctx_1024, 'L0_attn_norm_w': _L0_attn_in['norm_w'], 'L0_attn_in_proj_w': _L0_attn_in['in_proj_w'], 'L0_attn_conv_w': _L0_attn_in['conv_w'], 'L0_attn_conv_b': _L0_attn_in['conv_b'], 'L0_attn_x_proj_w': _L0_attn_in['x_proj_w'], 'L0_attn_dt_w': _L0_attn_in['dt_w'], 'L0_attn_dt_b': _L0_attn_in['dt_b'], 'L0_attn_A_log': _L0_attn_in['A_log'], 'L0_attn_Dp': _L0_attn_in['Dp'], 'L0_attn_out_w': _L0_attn_in['out_w'], 'L0_xattn_Wq': _L0_xattn_in['Wq'], 'L0_xattn_bq': _L0_xattn_in['bq'], 'L0_xattn_Wk': _L0_xattn_in['Wk'], 'L0_xattn_bk': _L0_xattn_in['bk'], 'L0_xattn_Wv': _L0_xattn_in['Wv'], 'L0_xattn_bv': _L0_xattn_in['bv'], 'L0_xattn_Wo': _L0_xattn_in['Wo'], 'L0_xattn_bo': _L0_xattn_in['bo'], 'L0_ffn_Wg': _L0_ffn_in['Wg'], 'L0_ffn_Wu': _L0_ffn_in['Wu'], 'L0_ffn_Wd': _L0_ffn_in['Wd'], 'L0_ffn_W1': _L0_ffn_in['W1'], 'L0_ffn_W2': _L0_ffn_in['W2']}

def reference(x, ctx_1024, L0_attn_norm_w, L0_attn_in_proj_w, L0_attn_conv_w, L0_attn_conv_b, L0_attn_x_proj_w, L0_attn_dt_w, L0_attn_dt_b, L0_attn_A_log, L0_attn_Dp, L0_attn_out_w, L0_xattn_Wq, L0_xattn_bq, L0_xattn_Wk, L0_xattn_bk, L0_xattn_Wv, L0_xattn_bv, L0_xattn_Wo, L0_xattn_bo, L0_ffn_Wg, L0_ffn_Wu, L0_ffn_Wd, L0_ffn_W1, L0_ffn_W2):
    import jax
    import jax.numpy as jnp

    def _L0_attn_ref(x, norm_w, in_proj_w, conv_w, conv_b, x_proj_w, dt_w, dt_b, A_log, Dp, out_w):
        import math
        import jax, jax.numpy as jnp
        import numpy as np
        from jax import lax
        D_MODEL = 256
        N_LAYERS = 2
        D_STATE = 16
        D_CONV = 4
        EXPAND = 2
        D_INNER = EXPAND * D_MODEL
        DT_RANK = math.ceil(D_MODEL / 16)
        BATCH = 2
        SEQLEN = 256
        BETA = 0.6
        ALPHA = 1.0
        EPS = 1e-05
        DT_MIN, DT_MAX, DT_FLOOR = (0.001, 0.1, 0.0001)

        def _rmsnorm(x, w):
            return x * jax.lax.rsqrt(jnp.mean(x * x, axis=-1, keepdims=True) + EPS) * w

        def _block(x, in_w, cw, cb, xp_w, dtw, dtb, a_log, dp, ow):
            B, L, _ = x.shape
            xz = jnp.einsum('bld,ed->ble', x, in_w)
            xb, z = jnp.split(xz, 2, axis=-1)
            xc = lax.conv_general_dilated(xb.transpose(0, 2, 1), cw[:, None, :], window_strides=(1,), padding=[(D_CONV - 1, 0)], dimension_numbers=('NCH', 'OIH', 'NCH'), feature_group_count=D_INNER)
            xb = jax.nn.silu((xc + cb[None, :, None]).transpose(0, 2, 1))
            dbc = jnp.einsum('ble,re->blr', xb, xp_w)
            delta = dbc[..., :DT_RANK]
            Bm = dbc[..., DT_RANK:DT_RANK + D_STATE]
            Cm = dbc[..., DT_RANK + D_STATE:]
            delta = jax.nn.softplus(jnp.einsum('blr,er->ble', delta, dtw) + dtb)
            dA = jnp.exp(delta[..., None] * -jnp.exp(a_log))
            mi = ALPHA * delta[..., None] * Bm[:, :, None, :] * xb[..., None]

            def scan_fn(carry, inp):
                h, v = carry
                dA_t, mi_t, C_t = inp
                v = BETA * v + mi_t
                h = dA_t * h + v
                y_t = jnp.einsum('ben,bn->be', h, C_t)
                return ((h, v), y_t)
            h0 = jnp.zeros((B, D_INNER, D_STATE), dtype=x.dtype)
            _, ys = lax.scan(scan_fn, (h0, h0), (dA.transpose(1, 0, 2, 3), mi.transpose(1, 0, 2, 3), Cm.transpose(1, 0, 2)))
            y = ys.transpose(1, 0, 2) + dp * xb
            y = y * jax.nn.silu(z)
            return jnp.einsum('ble,de->bld', y, ow)
        for i in range(N_LAYERS):
            x = x + _block(_rmsnorm(x, norm_w[i]), in_proj_w[i], conv_w[i], conv_b[i], x_proj_w[i], dt_w[i], dt_b[i], A_log[i], Dp[i], out_w[i])
        return x

    def _L0_xattn_ref(query_states, key_value_states, Wq, bq, Wk, bk, Wv, bv, Wo, bo):
        import jax, jax.numpy as jnp
        import numpy as np
        HIDDEN = 256
        NUM_HEADS = 16
        HEAD_DIM = HIDDEN // NUM_HEADS
        SCALE = 1.0 / float(np.sqrt(HEAD_DIM))
        B, SQ, _ = query_states.shape
        _, SKV, _ = key_value_states.shape
        q = query_states @ Wq.T + bq
        k = key_value_states @ Wk.T + bk
        v = key_value_states @ Wv.T + bv
        q = q.reshape(B, SQ, NUM_HEADS, HEAD_DIM).transpose(0, 2, 1, 3) * SCALE
        k = k.reshape(B, SKV, NUM_HEADS, HEAD_DIM).transpose(0, 2, 1, 3)
        v = v.reshape(B, SKV, NUM_HEADS, HEAD_DIM).transpose(0, 2, 1, 3)
        scores = jnp.einsum('bhqd,bhkd->bhqk', q, k)
        attn = jax.nn.softmax(scores, axis=-1)
        ctx = jnp.einsum('bhqk,bhkd->bhqd', attn, v)
        ctx = ctx.transpose(0, 2, 1, 3).reshape(B, SQ, HIDDEN)
        return ctx @ Wo.T + bo

    def _L0_ffn_ref(x, Wg, Wu, Wd, W1, W2):
        import jax, jax.numpy as jnp
        import numpy as np
        TOP_K = 2

        def _gelu(x):
            return jax.nn.gelu(x, approximate=False)
        B, S, D = x.shape
        E = Wu.shape[0]
        T = B * S
        xt = x.reshape(T, D)
        probs = jax.nn.softmax(xt @ Wg, axis=-1)
        topv, topi = jax.lax.top_k(probs, TOP_K)
        topv = topv / jnp.sum(topv, axis=-1, keepdims=True)
        cw = jnp.zeros((T, E), x.dtype).at[jnp.arange(T)[:, None], topi].set(topv)
        h = _gelu(jnp.einsum('td,edf->tef', xt, Wu))
        y = jnp.einsum('tef,efd->ted', h, Wd)
        moe = jnp.einsum('ted,te->td', y, cw)
        shared = _gelu(xt @ W1) @ W2
        return (shared + moe).reshape(B, S, D)
    x = x + _L0_attn_ref(_layernorm(x, axis=-1), L0_attn_norm_w, L0_attn_in_proj_w, L0_attn_conv_w, L0_attn_conv_b, L0_attn_x_proj_w, L0_attn_dt_w, L0_attn_dt_b, L0_attn_A_log, L0_attn_Dp, L0_attn_out_w)
    x = x + _L0_xattn_ref(_layernorm(x, axis=-1), ctx_1024, L0_xattn_Wq, L0_xattn_bq, L0_xattn_Wk, L0_xattn_bk, L0_xattn_Wv, L0_xattn_bv, L0_xattn_Wo, L0_xattn_bo)
    x = x + _L0_ffn_ref(_layernorm(x, axis=-1), L0_ffn_Wg, L0_ffn_Wu, L0_ffn_Wd, L0_ffn_W1, L0_ffn_W2)
    return x

_drawn_inputs = setup_inputs


def setup_inputs(seed=0):
    import zlib

    import numpy as np

    out = dict(_drawn_inputs(seed))
    spreads = {'L0_attn_norm_w': (1.0, 0.2),
     'L0_attn_conv_b': (0.0, 0.1),
     'L0_attn_Dp': (1.0, 0.2),
     'L0_xattn_bq': (0.0, 0.1),
     'L0_xattn_bk': (0.0, 0.1),
     'L0_xattn_bv': (0.0, 0.1),
     'L0_xattn_bo': (0.0, 0.1)}
    factors = {}
    for name, (base, spread) in spreads.items():
        noise = np.random.default_rng([zlib.crc32(name.encode()), seed]).standard_normal(out[name].shape)
        drawn = base * np.exp(spread * noise) if base else spread * noise
        out[name] = jnp.asarray(drawn.astype(out[name].dtype))
    for name, factor in factors.items():
        out[name] = (out[name] * factor).astype(out[name].dtype)
    return out
```

```python
from contextlib import ExitStack

import numpy as np

import concourse.bass as bass
from concourse import mybir

ALU = mybir.AluOpType
ACT = mybir.ActivationFunctionType
AX = mybir.AxisListType
F32 = mybir.dt.float32
U32 = mybir.dt.uint32
F32R = mybir.dt.float32r

P = 128
BETA = 0.6
EPS = 1e-5
NSTATE = 16
NTAP = 4
QC = P - NSTATE
HEADS, HDIM = 16, 16
HROW = 32
EXPERTS = 8
SP_MAX = 40.0


class Sem:

    def __init__(self, nc, ctx, name):
        self.handle = ctx.enter_context(nc.semaphore(name))
        self.count = 0


class Queue:

    def __init__(self, nc, ctx, name, engine):
        self.engine, self.waited = engine, {}
        self.sem = Sem(nc, ctx, "done_" + name)

    def wait(self, *marks):
        for m in marks:
            if m is None or self.waited.get(m[0], 0) >= m[1]:
                continue
            self.waited[m[0]] = m[1]
            self.engine.wait_ge(m[0].handle, m[1])

    def do(self, f):
        f(self.engine)

    def mark(self, f):
        self.sem.count += 1
        f(self.engine).then_inc(self.sem.handle, 1)
        return (self.sem, self.sem.count)

    def load(self, sem, f):
        sem.count += 16
        f(self.engine).then_inc(sem.handle, 16)
        return (sem, sem.count)

    def last(self):
        return (self.sem, self.sem.count) if self.sem.count else None


def build(nc, d, out, upto=3):
    B, S, D = d["x"].shape
    T = B * S
    NT, TB_, KD = T // P, S // P, D // P
    L = 2
    DI = d["conv_w"].shape[1]
    ET = DI // P
    RANK = 16
    NCH = -(-S // QC)
    CH = [min(QC, S - c * QC) for c in range(NCH)]
    WPAD = NCH * QC + NSTATE
    GN = 4
    F = d["W1"].shape[1]
    FT = F // P

    with ExitStack() as ctx:
        pe, dve, act, pool, sp = (
            Queue(nc, ctx, n, e) for n, e in (("tensor", nc.tensor), ("vector", nc.vector), ("scalar", nc.scalar),
                                              ("gpsimd", nc.gpsimd), ("sync", nc.sync)))
        ALLQ = (pe, dve, act, pool, sp)

        def sb(c, name, shape, dt=F32):
            return c.enter_context(nc.sbuf_tensor(name, shape, dt))

        def sem(name):
            return Sem(nc, ctx, name)

        def load(name, dst, src, *after):
            sp.wait(*after)
            return sp.load(sem("ld_" + name), lambda e: e.dma_start(dst, src))

        def phase_border():
            marks = [q.last() for q in ALLQ]
            for q in ALLQ:
                q.wait(*marks)

        psum = ctx.enter_context(nc.psum_tensor("psum", [P, 8, 512], F32))

        ident = sb(ctx, "ident", [P, P])
        xm = sb(ctx, "xm", [P, NT, D])
        stat = sb(ctx, "stat", [P, NT, 12])
        epst = sb(ctx, "epst", [P, 1])
        x_tok = d["x"].rearrange("b (t p) d -> p (b t) d", p=P)
        out_tok = out.rearrange("b (t p) d -> p (b t) d", p=P)

        ld_ident = load("ident", ident[:], d["ident"])
        ld_x = [load(f"x{b}", xm[:, b * TB_:(b + 1) * TB_, :], x_tok[:, b * TB_:(b + 1) * TB_, :]) for b in range(B)]
        m_eps = dve.mark(lambda e: e.memset(epst[:], EPS))

        def layernorm(b, src, src_marks, dst_free=None):
            tiles = range(b * TB_, (b + 1) * TB_)
            dve.wait(*src_marks)
            for t in tiles:
                dve.mark(lambda e, t=t: e.bn_stats(stat[:, t, 0:6], src[:, t, :]))
            dve.wait(dve.last())
            for t in tiles:
                m = dve.mark(lambda e, t=t: e.bn_aggr(stat[:, t, 6:8], stat[:, t, 0:6]))
            lo, hi = b * TB_, (b + 1) * TB_
            act.wait(m, m_eps)
            m = act.mark(lambda e: e.activation(stat[:, lo:hi, 8], stat[:, lo:hi, 7], ACT.Sqrt, bias=epst[:, 0:1]))
            dve.wait(m)
            m = dve.mark(lambda e: e.reciprocal(stat[:, lo:hi, 9], stat[:, lo:hi, 8]))
            dve.wait(m, dst_free)
            for t in tiles:
                m = dve.mark(lambda e, t=t: e.tensor_scalar(xm[:, t, :], src[:, t, :], stat[:, t, 6:7], stat[:, t, 9:10],
                                                            ALU.subtract, ALU.mult))
            return m

        with ExitStack() as mc:
            w_in = sb(mc, "w_in", [P, L, KD, 2 * DI])
            w_xp = sb(mc, "w_xp", [P, L, ET, RANK + 2 * NSTATE])
            w_dt = sb(mc, "w_dt", [RANK, L, DI])
            w_out = sb(mc, "w_out", [P, L, ET, D])
            w_cv = sb(mc, "w_cv", [P, L, ET, NTAP])
            vecs = sb(mc, "vecs", [P, L, 3, ET])
            normw = sb(mc, "normw", [P, L, KD])
            alog = sb(mc, "alog", [P, L, ET, NSTATE])
            aneg = sb(mc, "aneg", [P, L, ET, NSTATE])
            toep = sb(mc, "toep", [P, QC])
            keep = sb(mc, "keep", [P, 1])
            carry_id = sb(mc, "carry_id", [P, NCH, NSTATE])

            xs = sb(mc, "xs", [P, TB_, D])
            xnT = sb(mc, "xnT", [P, KD, S])
            xraw = sb(mc, "xraw", [P, ET, NTAP - 1 + S])
            uw = sb(mc, "uw", [P, ET, WPAD])
            xbs = sb(mc, "xbs", [P, 2, ET, WPAD])
            sz = sb(mc, "sz", [P, 2, ET, S])
            delta = sb(mc, "delta", [P, 2, ET, S])
            RBC = RANK + 2 * NSTATE
            dbc = sb(mc, "dbc", [RBC, WPAD])
            uT = sb(mc, "uT", [P, 2, NCH, DI])
            bcol = sb(mc, "bcol", [P, 2, NCH, NSTATE])
            bend = sb(mc, "bend", [P, NCH, NSTATE])
            ccol = sb(mc, "ccol", [P, 2, TB_, NSTATE])
            NG = NSTATE // GN
            filt = sb(mc, "filt", [P, 2, NCH, GN, QC])
            yacc = sb(mc, "yacc", [P, 2, TB_, DI])
            NDA, NH = 3, 9
            dA = sb(mc, "dA", [P, NDA, S])
            hst = sb(mc, "hst", [P, NH, S])

            wt = {}
            wt["w_in", 0] = load("w_in0", w_in[:, 0], d["w_in"][:, 0])
            for name, dst in (("normw", normw), ("w_cv", w_cv), ("vecs", vecs), ("w_xp", w_xp),
                              ("w_dt", w_dt), ("alog", alog), ("toep", toep), ("keep", keep), ("carry_id", carry_id),
                              ("w_out", w_out)):
                wt[name] = load(name, dst[:], d[name])
            wt["w_in", 1] = load("w_in1", w_in[:, 1], d["w_in"][:, 1])

            m_zero = [pool.mark(lambda e: e.memset(xraw[:], 0.0)), pool.mark(lambda e: e.memset(uw[:], 0.0)),
                      pool.mark(lambda e: e.memset(xbs[:], 0.0)), pool.mark(lambda e: e.memset(dbc[:], 0.0))]
            act.wait(wt["alog"])
            m = act.mark(lambda e: e.activation(aneg[:], alog[:], ACT.Exp))
            dve.wait(m)
            m_aneg = dve.mark(lambda e: e.tensor_scalar(aneg[:], aneg[:], -1.0, None, ALU.mult))

            v_free, t_free, x_free = [None] * 3, [None] * 3, [None] * 2
            cnt = {"v": 0, "t": 0, "x": 0, "a": 0, "h": 0}

            def bank(kind, base, free):
                i = cnt[kind] % len(free)
                cnt[kind] += 1
                pe.wait(free[i])
                return i, psum[:, base + i, :]

            def xbank():
                return bank("x", 6, x_free)

            def transpose4(dst, srcs):
                for j, s in enumerate(srcs):
                    f = lambda e, j=j, s=s: e.transpose(dst[:, j * P:(j + 1) * P], s, ident[:])
                    if j < len(srcs) - 1:
                        pe.do(f)
                return pe.mark(f)

            items = [(l, b) for l in range(L) for b in range(B)]
            n_items = len(items)
            stream = [None] * B
            for b in range(B):
                stream[b] = layernorm(b, xm, [ld_x[b]])
            done = [dict() for _ in range(n_items)]
            pe.wait(ld_ident)

            def front(k):
                l, b = items[k]
                par = k % 2
                me, old = done[k], done[k - 2] if k >= 2 else {}
                prev = done[k - 1] if k else {}
                t0 = b * TB_
                act.wait(stream[b], prev.get("xs_read"), m_eps)
                for t in range(TB_):
                    m = act.mark(lambda e: e.activation(xs[:, t, :], xm[:, t0 + t, :], ACT.Square,
                                                        accum_out=stat[:, t0 + t, 10:11]))
                act.wait(m)
                m = act.mark(lambda e: e.activation(stat[:, t0:t0 + TB_, 8], stat[:, t0:t0 + TB_, 10], ACT.Sqrt,
                                                    scale=1.0 / D, bias=epst[:, 0:1]))
                yield
                yield
                yield
                dve.wait(m)
                m = dve.mark(lambda e: e.reciprocal(stat[:, t0:t0 + TB_, 9], stat[:, t0:t0 + TB_, 8]))
                dve.wait(m)
                for t in range(TB_):
                    m = dve.mark(lambda e: e.tensor_scalar(xs[:, t, :], xm[:, t0 + t, :], stat[:, t0 + t, 9:10],
                                                           None, ALU.mult))
                yield
                pe.wait(m)
                for kt in range(KD):
                    i, bk = xbank()
                    me["xs_read"] = m = transpose4(bk, [xs[:, t, kt * P:(kt + 1) * P] for t in range(TB_)])
                    yield
                    dve.wait(m, prev.get("xnT_read"), wt["normw"])
                    x_free[i] = m_xn = dve.mark(lambda e: e.tensor_scalar(xnT[:, kt, :], bk, normw[:, l, kt:kt + 1],
                                                                          None, ALU.mult))
                yield

                def project(m8):
                    i, bk = xbank()
                    pe.wait(m_xn, wt["w_in", l])
                    for kt in range(KD):
                        f = lambda e: e.matmul(bk, w_in[:, l, kt, m8 * P:(m8 + 1) * P], xnT[:, kt, :],
                                               start=kt == 0, stop=kt == KD - 1)
                        m = pe.mark(f) if kt == KD - 1 else pe.do(f)
                    return i, bk, m

                for m4 in range(ET):
                    i, bk, m = project(m4)
                    yield
                    act.wait(m, *m_zero, prev.get("xraw_read"), prev.get("uw_read"), old.get("sz_read"), wt["w_cv"])
                    m_raw = act.mark(lambda e: e.copy(xraw[:, m4, NTAP - 1:], bk))
                    dst = uw[:, m4, NSTATE:NSTATE + S]
                    x_free[i] = m = act.mark(lambda e: e.activation(dst, bk, ACT.Identity, scale=w_cv[:, l, m4, NTAP - 1:NTAP]))
                    i, bk, m_z = project(ET + m4)
                    yield
                    for tap in range(NTAP - 1):
                        dve.wait(m)
                        m = dve.mark(lambda e: e.scalar_tensor_tensor(
                            out=dst, in0=xraw[:, m4, tap:tap + S], scalar=w_cv[:, l, m4, tap:tap + 1], in1=dst,
                            op0=ALU.mult, op1=ALU.add))
                    act.wait(m_z)
                    x_free[i] = act.mark(lambda e: e.copy(sz[:, par, m4, :], bk))
                me["conv"] = m
                act.wait(m, old.get("xbs_read"), wt["vecs"], x_free[i])
                for m4 in range(ET):
                    act.mark(lambda e: e.activation(sz[:, par, m4, :], sz[:, par, m4, :], ACT.Silu))
                    m = act.mark(lambda e: e.activation(xbs[:, par, m4, NSTATE:NSTATE + S], uw[:, m4, NSTATE:NSTATE + S],
                                                        ACT.Silu, bias=vecs[:, l, 0, m4:m4 + 1]))
                    if m4 == 1:
                        yield
                me["xnT_read"] = pe.last()
                me["sz"] = me["xbs"] = m
                yield
                i, bk = xbank()
                pe.wait(m, wt["w_xp"])
                for kt in range(ET):
                    f = lambda e: e.matmul(bk[0:RBC, :], w_xp[:, l, kt, :], xbs[:, par, kt, NSTATE:NSTATE + S],
                                           start=kt == 0, stop=kt == ET - 1)
                    m = pe.mark(f) if kt == ET - 1 else pe.do(f)
                yield
                act.wait(m, prev.get("dbc_read"))
                x_free[i] = m_dbc = act.mark(lambda e: e.copy(dbc[:, NSTATE:NSTATE + S], bk[0:RBC, :]))
                yield
                i, bk = xbank()
                pe.wait(m_dbc)
                starts = [c * QC for c in range(NCH)] + [NSTATE + t * P for t in range(TB_)]
                for j, w0 in enumerate(starts):
                    f = lambda e: e.transpose(bk[:, j * RBC:(j + 1) * RBC], dbc[:, w0:w0 + P], ident[0:RBC, 0:RBC])
                    m = pe.mark(f) if j == len(starts) - 1 else pe.do(f)
                yield
                dve.wait(m, wt["keep"], wt["carry_id"], old.get("bcol_read"), old.get("ccol_read"))
                tv = bk[:, 0:len(starts) * RBC].rearrange("p (j r) -> p j r", r=RBC)
                m = dve.mark(lambda e: e.scalar_tensor_tensor(
                    out=bcol[:, par], in0=tv[:, 0:NCH, RANK:RANK + NSTATE], scalar=keep[:, 0:1], in1=carry_id[:],
                    op0=ALU.mult, op1=ALU.add))
                me["bcol"] = m
                x_free[i] = me["ccol"] = dve.mark(lambda e: e.tensor_copy(ccol[:, par], tv[:, NCH:, RANK + NSTATE:]))
                dve.wait(m, wt["toep"], prev.get("bend_read"))
                m_bend = dve.mark(lambda e: e.tensor_scalar(bend[:], bcol[:, par], toep[:, QC - 1:QC], None, ALU.mult))
                for m4 in range(ET):
                    i, bk = xbank()
                    pe.wait(m_dbc, wt["w_dt"])
                    m = pe.mark(lambda e: e.matmul(bk, w_dt[:, l, m4 * P:(m4 + 1) * P], dbc[0:RANK, NSTATE:NSTATE + S], start=True, stop=True))
                    yield
                    act.wait(m, old.get("delta_read"), me["conv"])
                    x_free[i] = m = act.mark(lambda e: e.activation(delta[:, par, m4, :], bk, ACT.Identity, bias=vecs[:, l, 1, m4:m4 + 1]))
                me["dbc_read"] = pe.last()
                yield
                dve.wait(m)
                m = dve.mark(lambda e: e.tensor_scalar(xraw[:, :, NTAP - 1:], delta[:, par], SP_MAX, None, ALU.min))
                yield
                for part in range(2):
                    act.wait(m)
                    xr2 = xraw[:, 2 * part:2 * part + 2, NTAP - 1:]
                    m2 = act.mark(lambda e: e.activation(xr2, xr2, ACT.Exp))
                    act.wait(m2)
                    m2 = act.mark(lambda e: e.activation(xr2, xr2, ACT.Ln, bias=1.0))
                    yield
                yield
                yield
                for m4 in range(ET):
                    dve.wait(m2)
                    m = dve.mark(lambda e: e.tensor_tensor(delta[:, par, m4, :], delta[:, par, m4, :], xraw[:, m4, NTAP - 1:], ALU.max))
                    pool.wait(m, me["xbs"], *m_zero)
                    m_u = pool.mark(lambda e: e.tensor_tensor(uw[:, m4, NSTATE:NSTATE + S], delta[:, par, m4, :],
                                                              xbs[:, par, m4, NSTATE:NSTATE + S], ALU.mult))
                    yield
                me["delta"] = me["xraw_read"] = m
                for c in range(NCH):
                    i, bk = xbank()
                    pe.wait(m_u)
                    m = transpose4(bk, [uw[:, et, c * QC:c * QC + P] for et in range(ET)])
                    yield
                    act.wait(m, old.get("uT_read"))
                    x_free[i] = m_uT = act.mark(lambda e: e.copy(uT[:, par, c, :], bk))
                me["uw_read"] = pe.last()
                for c in range(NCH - 1):
                    yield
                    i, bk = xbank()
                    pe.wait(m_bend, m_uT)
                    m = pe.mark(lambda e: e.matmul(bk[0:NSTATE, :], bend[:, c, :], uT[:, par, c, :], start=True, stop=True))
                    yield
                    act.wait(m, m_uT)
                    x_free[i] = m_uT = act.mark(lambda e: e.copy(uT[0:NSTATE, par, c + 1, :], bk[0:NSTATE, :]))
                me["bend_read"] = pe.last()
                me["uT"] = m_uT

            g_state = {"n": 0}
            filt_free = [None, None]

            def build_filter(k, g):
                slot = g_state["n"] % 2
                g_state["n"] += 1
                pool.wait(done[k]["bcol"], wt["toep"], filt_free[slot])
                par = k % 2
                m = pool.mark(lambda e: e.tensor_tensor(
                    filt[:, slot], toep[:, :].unsqueeze(1).unsqueeze(1).to_broadcast([P, NCH, GN, QC]),
                    bcol[:, par, :, g * GN:(g + 1) * GN].unsqueeze(3).to_broadcast([P, NCH, GN, QC]), ALU.mult))
                done[k]["bcol_read"] = m
                return slot, m

            dA_free, h_free = [None] * NDA, [None] * NH
            y_free = [None, None]
            ready_filter = {}

            def add_state(k, n, hs, t):
                par, me = k % 2, done[k]
                i, bk = bank("t", 3, t_free)
                pe.wait(hs[-1][1])
                m = transpose4(bk, [hst[:, s, t * P:(t + 1) * P] for s, _ in hs])
                c = ccol[:, par, t, n:n + 1]
                if n == 0:
                    dve.wait(m, y_free[par], me["ccol"])
                    f = lambda e: e.tensor_scalar(yacc[:, par, t, :], bk, c, None, ALU.mult)
                else:
                    dve.wait(m, me["y", t])
                    f = lambda e: e.scalar_tensor_tensor(out=yacc[:, par, t, :], in0=bk, scalar=c, in1=yacc[:, par, t, :],
                                                         op0=ALU.mult, op1=ALU.add)
                me["y", t] = t_free[i] = dve.mark(f)
                if t == TB_ - 1:
                    for s, _ in hs:
                        h_free[s] = pe.last()
                    if n == NSTATE - 1:
                        me["ccol_read"] = t_free[i]

            def main(k, pend, side):
                l, b = items[k]
                par = k % 2
                me = done[k]
                for n in range(NSTATE):
                    g = n // GN
                    slot, m_f = ready_filter[k, g]
                    if n % GN == 0 and g + 1 < NG:
                        ready_filter[k, g + 1] = build_filter(k, g + 1)
                    if g == NG - 1 and k + 1 < n_items and (k + 1, 0) not in ready_filter and "bcol" in done[k + 1]:
                        ready_filter[k + 1, 0] = build_filter(k + 1, 0)
                    hs = []
                    for et in range(ET):
                        i, bk = bank("v", 0, v_free)
                        pe.wait(m_f, me["uT"])
                        for c in range(NCH):
                            f = lambda e: e.matmul(bk[:, c * QC:c * QC + CH[c]], uT[:, par, c, et * P:(et + 1) * P],
                                                   filt[:, slot, c, n % GN, 0:CH[c]], start=True, stop=True)
                            m_v = pe.mark(f) if c == NCH - 1 else pe.do(f)
                        a = cnt["a"] % NDA
                        cnt["a"] += 1
                        act.wait(dA_free[a], me["delta"], m_aneg)
                        m_a = act.mark(lambda e: e.activation(dA[:, a, :], delta[:, par, et, :], ACT.Exp,
                                                              scale=aneg[:, l, et, n:n + 1]))
                        s = cnt["h"] % NH
                        cnt["h"] += 1
                        dve.wait(m_v, m_a, h_free[s])
                        m_h = dve.mark(lambda e: e.tensor_tensor_scan(hst[:, s, :], dA[:, a, :], bk, 0.0, ALU.mult, ALU.add))
                        v_free[i] = dA_free[a] = m_h
                        hs.append((s, m_h))
                        if pend is not None:
                            add_state(*pend, et)
                        next(side, None)
                    if n % GN == GN - 1:
                        filt_free[slot] = pe.last()
                    pend = (k, n, hs)
                me["uT_read"], me["delta_read"] = pe.last(), act.last()
                for _ in side:
                    pass
                if k + 1 < n_items and (k + 1, 0) not in ready_filter:
                    ready_filter[k + 1, 0] = build_filter(k + 1, 0)
                return pend

            def back(k):
                l, b = items[k]
                par = k % 2
                me = done[k]
                for et in range(ET):
                    i, bk = xbank()
                    pe.wait(*[me["y", t] for t in range(TB_)])
                    m = transpose4(bk, [yacc[:, par, t, et * P:(et + 1) * P] for t in range(TB_)])
                    yield
                    dve.wait(m, me["xbs"])
                    xd = xbs[:, par, et, NSTATE:NSTATE + S]
                    x_free[i] = m = dve.mark(lambda e: e.scalar_tensor_tensor(
                        out=xd, in0=xd, scalar=vecs[:, l, 2, et:et + 1], in1=bk, op0=ALU.mult, op1=ALU.add))
                    pool.wait(m, me["sz"])
                    m_g = pool.mark(lambda e: e.tensor_tensor(sz[:, par, et, :], sz[:, par, et, :], xd, ALU.mult))
                y_free[par] = pe.last()
                me["xbs_read"] = m_g
                yield
                yield
                for t in range(TB_):
                    i, bk = xbank()
                    pe.wait(m_g, wt["w_out"])
                    for kt in range(ET):
                        f = lambda e: e.matmul(bk[:, 0:D], sz[:, par, kt, t * P:(t + 1) * P], w_out[:, l, kt, :],
                                               start=kt == 0, stop=kt == ET - 1)
                        m = pe.mark(f) if kt == ET - 1 else pe.do(f)
                    yield
                    dve.wait(m)
                    x_free[i] = dve.mark(lambda e: e.tensor_tensor(xm[:, b * TB_ + t, :], xm[:, b * TB_ + t, :], bk[:, 0:D], ALU.add))
                me["sz_read"] = pe.last()
                stream[b] = dve.last()

            def sides(k):
                for _ in range(ET):
                    yield
                if k:
                    yield from back(k - 1)
                if k + 1 < n_items:
                    yield from front(k + 1)

            for _ in front(0):
                pass
            ready_filter[0, 0] = build_filter(0, 0)
            pend = None
            for k in range(n_items):
                pend = main(k, pend, sides(k))
            for t in range(TB_):
                add_state(*pend, t)
            for _ in back(n_items - 1):
                pass
        phase_border()

        xres = sb(ctx, "xres", [P, NT, D])
        m_x1 = []
        for b in range(B):
            r = xres[:, b * TB_:(b + 1) * TB_, :]
            dve.wait(load(f"xres{b}", r, x_tok[:, b * TB_:(b + 1) * TB_, :]))
            m_x1.append(dve.mark(lambda e: e.tensor_tensor(r, r, xm[:, b * TB_:(b + 1) * TB_, :], ALU.add)))

        if upto >= 2:
            with ExitStack() as ac:
                HG = HEADS // 4
                UH = HEADS // 2
                UG = UH // 4
                w_q = sb(ac, "w_q", [P, KD, HG, P])
                w_k = sb(ac, "w_k", [P, KD, HG, P])
                w_v = sb(ac, "w_v", [P, KD, HEADS * HROW])
                w_o = sb(ac, "w_o", [P, HG, D])
                b_qk = sb(ac, "b_qk", [P, 2, HG])
                b_v = sb(ac, "b_v", [P, HEADS * HROW])
                b_o = sb(ac, "b_o", [P, D])
                spread = sb(ac, "spread", [P, P])
                ctxT = sb(ac, "ctxT", [P, 2, KD, S])
                xnT = sb(ac, "axnT", [P, KD, S])
                flat = sb(ac, "flat", [P, 2, S])
                part = sb(ac, "part", [P, 2, 2, UG, S], F32R)
                qk = sb(ac, "qk", [P, 2, 2, UH, S], F32R)
                vt = sb(ac, "vt", [P, 2, TB_, HEADS * HROW])
                nmax = sb(ac, "nmax", [P, 2, TB_, UH])
                nsplit = sb(ac, "nsplit", [P, 2, TB_, 2 * UH], F32R)
                nrow = sb(ac, "nrow", [2 * UH, 2, S], F32R)
                NPT = 2
                pT = sb(ac, "pT", [P, NPT, 4, S])
                oT = sb(ac, "oT", [P, HG, S])
                rc = sb(ac, "rc", [P, S])
                aw = {n: load(n, t[:], d[n]) for n, t in (("w_q", w_q), ("w_k", w_k), ("w_v", w_v), ("w_o", w_o),
                      ("b_qk", b_qk), ("spread", spread))}
                aw["b_v"] = load("b_v", b_v[:], d["b_v"].partition_broadcast(P))
                aw["b_o"] = load("b_o", b_o[:], d["b_o"].partition_broadcast(P))
                ld_ctx = [load(f"ctx{b}", ctxT[:, b], d["ctxT"][b]) for b in range(2)]
                s_strip = [sem("strips0"), sem("strips1")]
                s_rows = [sem("rows0"), sem("rows1")]
                pair_free, pv_free, one_free = [None] * 3, [None], [None]
                pc = {"n": 0, "p": 0, "f": 0}
                pT_free, flat_free = [None] * NPT, [None, None]
                ctx_read, vt_read, oT_read, xnT_read, rc_read = [None, None], [None, None], [None], [None], [None]
                ud = [dict() for _ in range(2 * B)]
                m_v, m_x2, m_div = [None] * B, [None] * B, {}

                def one(f_list):
                    pe.wait(one_free[0])
                    for f in f_list[:-1]:
                        pe.do(f)
                    return pe.mark(f_list[-1])

                def prepare(u):
                    b, half = divmod(u, 2)
                    cp, par, me = b % 2, u % 2, ud[u]
                    prev, old = (ud[u - 1] if u else {}), (ud[u - 2] if u > 1 else {})
                    if half == 0:
                        ln = layernorm(b, xres, [m_x1[b]])
                        yield
                        yield
                        for kt in range(KD):
                            pe.wait(ln)
                            m = one([lambda e, t=t: e.transpose(psum[:, 7, t * P:(t + 1) * P], xm[:, b * TB_ + t, kt * P:(kt + 1) * P], ident[:])
                                     for t in range(TB_)])
                            yield
                            dve.wait(m, xnT_read[0])
                            one_free[0] = me["xn"] = dve.mark(lambda e: e.tensor_copy(xnT[:, kt, :], psum[:, 7, :]))
                    else:
                        me["xn"] = prev["xn"]
                    for g in range(UG):
                        for which, w, src, ready in ((1, w_k, ctxT[:, cp], ld_ctx[b]), (0, w_q, xnT, me["xn"])):
                            hg = half * UG + g
                            pe.wait(aw["w_k"], aw["w_q"], ready)
                            m = one([lambda e, kt=kt: e.matmul(psum[:, 7, :], w[:, kt, hg, :], src[:, kt, :], start=kt == 0, stop=kt == KD - 1)
                                     for kt in range(KD)])
                            yield
                            z = pc["f"] % 2
                            pc["f"] += 1
                            dve.wait(m, aw["b_qk"], flat_free[z])
                            one_free[0] = m = dve.mark(lambda e: e.tensor_scalar(flat[:, z, :], psum[:, 7, :], b_qk[:, which, hg:hg + 1], None, ALU.add))
                            dve.wait(m, prev.get("part_read"))
                            hi, lo = part[:, which, 0, g, :], part[:, which, 1, g, :]
                            m = dve.mark(lambda e: e.tensor_copy(hi, flat[:, z, :]))
                            dve.wait(m)
                            flat_free[z] = m = dve.mark(lambda e: e.tensor_tensor(lo, flat[:, z, :], hi.bitcast(F32), ALU.subtract))
                    if half:
                        xnT_read[0] = pe.last()
                    sp.wait(m, old.get("qk_read"))
                    for which, order in ((1, (0, 1, 0, 1)), (0, (0, 0, 1, 1))):
                        for i in range(4):
                            for strip, p in enumerate(order):
                                dst = qk[strip * HROW:(strip + 1) * HROW, par, which, i::4, :]
                                src = part[i * HROW:(i + 1) * HROW, which, p, :, :]
                                me["strips"] = sp.load(s_strip[par], lambda e: e.dma_start(dst.bitcast(F32), src.bitcast(F32)))
                    me["part_read"] = me["strips"]
                    if half == 0:
                        for kv in range(TB_):
                            pe.wait(aw["w_v"], ld_ctx[b])
                            m = one([lambda e, kt=kt: e.matmul(psum[:, 7, :], ctxT[:, cp, kt, kv * P:(kv + 1) * P], w_v[:, kt, :],
                                                               start=kt == 0, stop=kt == KD - 1) for kt in range(KD)])
                            yield
                            dve.wait(m, aw["b_v"], vt_read[cp])
                            one_free[0] = m_v[b] = dve.mark(lambda e: e.tensor_tensor(vt[:, cp, kv, :], psum[:, 7, :], b_v[:], ALU.add))
                    else:
                        ctx_read[cp] = pe.last()
                        if b + 2 < B:
                            ld_ctx.append(load(f"ctx{b + 2}", ctxT[:, cp], d["ctxT"][b + 2], ctx_read[cp]))

                def pair(mms):
                    i = pc["n"] % 3
                    pc["n"] += 1
                    pe.wait(pair_free[i])
                    pe.do(lambda e: mms[0](e, psum[:, 2 * i, :]))
                    return i, pe.mark(lambda e: mms[1](e, psum[:, 2 * i + 1, :]))

                def maxima(u):
                    par, me = u % 2, ud[u]
                    old = ud[u - 2] if u > 1 else {}
                    q, k = qk[:, par, 0], qk[:, par, 1]
                    for h in range(0, UH, 2):
                        for t in range(TB_):
                            pe.wait(me["strips"])
                            i, m = pair([lambda e, o, h=h + j: e.matmul(o, q[:, h, t * P:(t + 1) * P], k[:, h, :], start=True, stop=True)
                                         for j in range(2)])
                            dve.wait(m, old.get("nmax_read"))
                            pair_free[i] = m = dve.mark(lambda e: e.tensor_reduce(nmax[:, par, t, h:h + 2], psum[:, 2 * i:2 * i + 2, :], AX.X,
                                                                                  ALU.max, negate=True))
                            if t % 2:
                                yield
                    dve.wait(m, old.get("nsplit_read"))
                    m = dve.mark(lambda e: e.tensor_copy(nsplit[:, par, :, 0:UH], nmax[:, par]))
                    dve.wait(m)
                    m = dve.mark(lambda e: e.tensor_tensor(nsplit[:, par, :, UH:], nmax[:, par], nsplit[:, par, :, 0:UH].bitcast(F32), ALU.subtract))
                    me["nmax_read"] = m
                    yield
                    pe.wait(m, ld_ident)
                    m = one([lambda e, t=t: e.transpose(psum[0:2 * UH, 7, t * P:(t + 1) * P], nsplit[:, par, t, :].bitcast(F32), ident[:])
                             for t in range(TB_)])
                    me["nsplit_read"] = m
                    yield
                    dve.wait(m, old.get("rows"))
                    one_free[0] = m = dve.mark(lambda e: e.tensor_copy(nrow[:, par, :], psum[0:2 * UH, 7, :]))
                    sp.wait(m)
                    for p in range(2):
                        r = 2 * p * HROW + HDIM
                        me["rows"] = sp.load(s_rows[par], lambda e: e.dma_start(qk[r:r + 1, par, 0, :, :].bitcast(F32),
                                                                         nrow[p * UH:(p + 1) * UH, par, :].bitcast(F32)))

                def weighted(u, side):
                    b, half = divmod(u, 2)
                    par, cp, me = u % 2, b % 2, ud[u]
                    q, k = qk[:, par, 0], qk[:, par, 1]

                    def values(g, kv, z, m_e):
                        hg = half * UG + g
                        pe.wait(m_e, m_v[b], pv_free[0])
                        for i in range(4):
                            c0 = (hg * 4 + i) * HROW
                            f = lambda e: e.matmul(psum[i * HROW:(i + 1) * HROW, 6, :], vt[:, cp, kv, c0:c0 + HROW], pT[:, z, i, :],
                                                   start=kv == 0, stop=kv == TB_ - 1, tile_position=(0, i * HROW))
                            m = pe.mark(f) if i == 3 else pe.do(f)
                        pT_free[z] = m
                        if kv == TB_ - 1:
                            dve.wait(m, oT_read[0])
                            pv_free[0] = m_div[hg] = dve.mark(lambda e: e.tensor_copy(oT[:, hg, :], psum[:, 6, :]))

                    def divide(g):
                        hg = half * UG + g
                        pe.wait(m_div[hg], aw["spread"])
                        m = one([lambda e: e.matmul(psum[:, 7, :], spread[:], oT[:, hg, :], start=True, stop=True)])
                        dve.wait(m, rc_read[0])
                        one_free[0] = m = dve.mark(lambda e: e.reciprocal(rc[:], psum[:, 7, :]))
                        dve.wait(m)
                        m_div[hg] = rc_read[0] = dve.mark(lambda e: e.tensor_tensor(oT[:, hg, :], oT[:, hg, :], rc[:], ALU.mult))

                    before = None
                    for g in range(UG):
                        for kv in range(TB_):
                            z = pc["p"] % NPT
                            pc["p"] += 1
                            for hp in range(2):
                                pe.wait(me["rows"])
                                i, m = pair([lambda e, o, h=4 * g + 2 * hp + j: e.matmul(o, k[:, h, kv * P:(kv + 1) * P], q[:, h, :], start=True, stop=True)
                                             for j in range(2)])
                                act.wait(m, pT_free[z])
                                pair_free[i] = m_e = act.mark(lambda e: e.activation(pT[:, z, 2 * hp:2 * hp + 2], psum[:, 2 * i:2 * i + 2, :], ACT.Exp,
                                                                                     scale=HDIM ** -0.5))
                            for _ in range(4):
                                next(side, None)
                            if before is not None:
                                values(*before)
                                if before[1] == TB_ - 1:
                                    divide(before[0])
                            before = (g, kv, z, m_e)
                    me["qk_read"] = pe.last()
                    values(*before)
                    divide(UG - 1)
                    for _ in side:
                        pass
                    if half:
                        vt_read[cp] = pe.last()

                def project_out(b):
                    for t in range(TB_):
                        pe.wait(aw["w_o"], *m_div.values())
                        m = one([lambda e, hg=hg: e.matmul(psum[:, 7, 0:D], oT[:, hg, t * P:(t + 1) * P], w_o[:, hg, :], start=hg == 0, stop=hg == HG - 1)
                                 for hg in range(HG)])
                        dve.wait(m, aw["b_o"])
                        r = xres[:, b * TB_ + t, :]
                        one_free[0] = m = dve.mark(lambda e: e.tensor_tensor(r, r, psum[:, 7, 0:D], ALU.add))
                        dve.wait(m)
                        m_x2[b] = dve.mark(lambda e: e.tensor_tensor(r, r, b_o[:], ALU.add))
                    oT_read[0] = pe.last()

                def alternate(*parts):
                    parts = list(parts)
                    while parts:
                        for g in list(parts):
                            if next(g, g) is g:
                                parts.remove(g)
                            else:
                                yield

                NU = 2 * B
                for _ in prepare(0):
                    pass
                for _ in alternate(maxima(0), prepare(1)):
                    pass
                for u in range(NU):
                    side = [maxima(u + 1)] if u + 1 < NU else []
                    weighted(u, alternate(*side))
                    if u % 2:
                        project_out(u // 2)
                    if u + 2 < NU:
                        for _ in prepare(u + 2):
                            pass
            phase_border()

        if upto >= 3:
            with ExitStack() as fc:
                w_g = sb(fc, "w_g", [P, KD, EXPERTS])
                raw = sb(fc, "raw", [P, 2, 2, KD * F])
                wh = sb(fc, "wh", [P, 2, 2, KD * F], F32R)
                wl = sb(fc, "wl", [P, 2, 2, KD * F], F32R)
                xn = sb(fc, "xn", [P, 2, KD, S])
                xh = sb(fc, "xh", [P, B, KD, S], F32R)
                xl = sb(fc, "xl", [P, B, KD, S], F32R)
                NHB = 2
                h32 = sb(fc, "h32", [P, NHB, FT, S])
                hh = sb(fc, "hh", [P, NHB, FT, S], F32R)
                hl = sb(fc, "hl", [P, NHB, FT, S], F32R)
                gate = sb(fc, "gate", [P, NT, 48])
                gidx = sb(fc, "gidx", [P, NT, 8], U32)
                iota = sb(fc, "iota", [P, EXPERTS])
                order = [EXPERTS] + list(range(EXPERTS))
                raw_ld, raw_read, w_ready, w_read = {}, [None, None], {}, [None, None]

                def load_expert(j):
                    x, z = order[j], j % 2
                    raw_ld[j] = [load(f"up{x}", raw[:, z, 0].rearrange("p (k f) -> p k f", k=KD), d["up"][x], raw_read[z]),
                                 load(f"down{x}", raw[:, z, 1].rearrange("p (k f) -> p k f", k=FT), d["down"][x], raw_read[z])]

                def split_expert(j):
                    z = j % 2
                    pool.wait(*raw_ld[j], w_read[z])
                    for half in range(2):
                        m = pool.mark(lambda e: e.tensor_copy(wh[:, z, half], raw[:, z, half]))
                        pool.wait(m)
                        m = pool.mark(lambda e: e.tensor_tensor(wl[:, z, half], raw[:, z, half], wh[:, z, half].bitcast(F32), ALU.subtract))
                    w_ready[j] = raw_read[z] = m

                ld_wg = load("w_g", w_g[:], d["w_g"])
                ld_iota = load("iota", iota[:], d["iota"])
                load_expert(0)
                load_expert(1)
                split_expert(0)

                hid_free, out_free, tr_free = [None] * 4, [None] * 3, [None]
                c3 = {"h": 0, "o": 0}
                h_free = [None] * NHB
                xn_read = [None, None]
                m_x, m_cw = [None] * B, [None] * B
                m_res = [None] * NT

                def normalise(b):
                    par = b % 2
                    ln = layernorm(b, xres, [m_x2[b]], None)
                    for kt in range(KD):
                        pe.wait(ln, tr_free[0])
                        for t in range(TB_):
                            f = lambda e: e.transpose(psum[:, 7, t * P:(t + 1) * P], xm[:, b * TB_ + t, kt * P:(kt + 1) * P], ident[:])
                            m = pe.mark(f) if t == TB_ - 1 else pe.do(f)
                        act.wait(m, xn_read[par])
                        tr_free[0] = m = act.mark(lambda e: e.copy(xn[:, par, kt, :], psum[:, 7, :]))
                        dve.wait(m)
                        m = dve.mark(lambda e: e.tensor_copy(xh[:, b, kt, :], xn[:, par, kt, :]))
                        dve.wait(m)
                        m_x[b] = dve.mark(lambda e: e.tensor_tensor(xl[:, b, kt, :], xn[:, par, kt, :], xh[:, b, kt, :].bitcast(F32), ALU.subtract))

                def route(b):
                    par = b % 2
                    lo, hi = b * TB_, (b + 1) * TB_
                    pe.wait(m_x[b], ld_wg, tr_free[0])
                    for t in range(TB_):
                        for kt in range(KD):
                            f = lambda e: e.matmul(psum[:, 7, t * EXPERTS:(t + 1) * EXPERTS],
                                                   xn[:, par, kt, t * P:(t + 1) * P], w_g[:, kt, :],
                                                   start=kt == 0, stop=kt == KD - 1)
                            m = pe.mark(f) if (t, kt) == (TB_ - 1, KD - 1) else pe.do(f)
                    xn_read[par] = m
                    lg = psum[:, 7, 0:TB_ * EXPERTS].rearrange("p (t x) -> p t x", x=EXPERTS)
                    G = gate[:, lo:hi, :]
                    bc = lambda c: G[:, :, c:c + 1].to_broadcast([P, TB_, EXPERTS])
                    dve.wait(m, ld_iota)
                    m = dve.mark(lambda e: e.tensor_reduce(G[:, :, 40], lg, AX.X, ALU.max))
                    dve.wait(m)
                    tr_free[0] = m = dve.mark(lambda e: e.tensor_tensor(G[:, :, 0:8], lg, bc(40), ALU.subtract))
                    act.wait(m)
                    m = act.mark(lambda e: e.activation(G[:, :, 0:8], G[:, :, 0:8], ACT.Exp))
                    dve.wait(m)
                    m = dve.mark(lambda e: e.tensor_reduce(G[:, :, 41], G[:, :, 0:8], AX.X, ALU.add))
                    dve.wait(m)
                    m = dve.mark(lambda e: e.reciprocal(G[:, :, 42], G[:, :, 41]))
                    dve.wait(m)
                    m = dve.mark(lambda e: e.tensor_tensor(G[:, :, 0:8], G[:, :, 0:8], bc(42), ALU.mult))
                    dve.wait(m)
                    for t in range(lo, hi):
                        m = dve.mark(lambda e: e.max(gate[:, t, 8:16], gate[:, t, 0:8]))
                    dve.wait(m)
                    for t in range(lo, hi):
                        m = dve.mark(lambda e: e.max_index(gidx[:, t, :], gate[:, t, 8:16], gate[:, t, 0:8]))
                    m2 = dve.mark(lambda e: e.tensor_tensor(G[:, :, 43], G[:, :, 8], G[:, :, 9], ALU.add))
                    dve.wait(m, m2)
                    m = dve.mark(lambda e: e.reciprocal(G[:, :, 44], G[:, :, 43]))
                    m2 = dve.mark(lambda e: e.tensor_copy(G[:, :, 46:48], gidx[:, lo:hi, 0:2]))
                    dve.wait(m, m2)
                    m = dve.mark(lambda e: e.tensor_tensor(G[:, :, 16:18], G[:, :, 8:10], G[:, :, 44:45].to_broadcast([P, TB_, 2]), ALU.mult))
                    dve.wait(m)
                    for t in range(lo, hi):
                        for j in range(2):
                            m = dve.mark(lambda e: e.tensor_scalar(gate[:, t, 24 + 8 * j:32 + 8 * j], iota[:],
                                                                   gate[:, t, 46 + j:47 + j], gate[:, t, 16 + j:17 + j],
                                                                   ALU.is_equal, ALU.mult))
                    dve.wait(m)
                    m_cw[b] = dve.mark(lambda e: e.tensor_tensor(G[:, :, 24:32], G[:, :, 24:32], G[:, :, 32:40], ALU.add))

                def three(dst, ah, al, bh, bl, first, last):
                    for n, (p, q) in enumerate(((ah, bh), (al, bh), (ah, bl))):
                        f = lambda e: e.matmul(dst, p, q, start=first and n == 0, stop=last and n == 2)
                        m = pe.mark(f) if last and n == 2 else pe.do(f)
                    return m

                def hidden(j, b, hz):
                    z = j % 2
                    pe.wait(w_ready[j], m_x[b])
                    for ft in range(FT):
                        i = c3["h"] % 4
                        c3["h"] += 1
                        pe.wait(hid_free[i])
                        for kt in range(KD):
                            w0 = kt * F + ft * P
                            m = three(psum[:, i, :], wh[:, z, 0, w0:w0 + P], wl[:, z, 0, w0:w0 + P], xh[:, b, kt, :], xl[:, b, kt, :],
                                      kt == 0, kt == KD - 1)
                        act.wait(m, h_free[hz])
                        hid_free[i] = m = act.mark(lambda e: e.activation(h32[:, hz, ft, :], psum[:, i, :], ACT.Gelu))
                        dve.wait(m, h_free[hz])
                        m = dve.mark(lambda e: e.tensor_copy(hh[:, hz, ft, :], h32[:, hz, ft, :]))
                        dve.wait(m)
                        m = dve.mark(lambda e: e.tensor_tensor(hl[:, hz, ft, :], h32[:, hz, ft, :], hh[:, hz, ft, :].bitcast(F32), ALU.subtract))
                    return m

                def outputs(j, b, hz, m_h):
                    x, z = order[j], j % 2
                    pe.wait(m_h)
                    for t in range(TB_):
                        i = c3["o"] % 3
                        c3["o"] += 1
                        pe.wait(out_free[i])
                        for ft in range(FT):
                            w0 = ft * D
                            m = three(psum[:, 4 + i, 0:D], hh[:, hz, ft, t * P:(t + 1) * P], hl[:, hz, ft, t * P:(t + 1) * P],
                                      wh[:, z, 1, w0:w0 + D], wl[:, z, 1, w0:w0 + D], ft == 0, ft == FT - 1)
                        tt = b * TB_ + t
                        r = xres[:, tt, :]
                        if x == EXPERTS:
                            dve.wait(m)
                            g = lambda e: e.tensor_tensor(r, r, psum[:, 4 + i, 0:D], ALU.add)
                        else:
                            dve.wait(m, m_res[tt], m_cw[b])
                            g = lambda e: e.scalar_tensor_tensor(out=r, in0=psum[:, 4 + i, 0:D], scalar=gate[:, tt, 24 + x:25 + x],
                                                                 in1=r, op0=ALU.mult, op1=ALU.add)
                        m_res[tt] = out_free[i] = dve.mark(g)
                    h_free[hz] = pe.last()

                stored = []
                normalise(0)
                steps = [(j, b) for j in range(len(order)) for b in range(B)]
                before = None
                for n, (j, b) in enumerate(steps):
                    if b == 1 and j + 1 < len(order):
                        split_expert(j + 1)
                    if j == 0 and b + 1 < B:
                        normalise(b + 1)
                    m_h = hidden(j, b, n % NHB)
                    if b == 1 and j + 2 < len(order):
                        load_expert(j + 2)
                    if j == 0:
                        route(b)
                    if before is not None:
                        outputs(*before)
                        if before[1] == B - 1:
                            w_read[before[0] % 2] = pe.last()
                    before = (j, b, n % NHB, m_h)
                outputs(*before)

        s_out = sem("stored")
        for b in range(B):
            sp.wait(m_res[(b + 1) * TB_ - 1] if upto >= 3 else dve.last())
            m = sp.load(s_out, lambda e, b=b: e.dma_start(out_tok[:, b * TB_:(b + 1) * TB_, :], xres[:, b * TB_:(b + 1) * TB_, :]))
        sp.wait(m)


def shape_constants():
    f = np.float32
    toep = np.zeros((P, QC), np.float64)
    toep[:NSTATE] = BETA ** (np.arange(QC) + 1)
    for s in range(QC):
        toep[NSTATE + s, s:] = BETA ** np.arange(QC - s)
    keep = (np.arange(P) >= NSTATE).astype(f)[:, None]
    n_chunks = -(-512 // QC)
    carry_id = np.zeros((P, n_chunks, NSTATE), f)
    carry_id[:NSTATE] = np.eye(NSTATE, dtype=f)[:, None, :]
    spread = np.zeros((P, P), f)
    for h in range(4):
        spread[HROW * h + HDIM, HROW * h:HROW * (h + 1)] = 1
    return {"toep": toep.astype(f), "keep": keep, "carry_id": carry_id, "spread": spread,
            "ident": np.eye(P, dtype=f), "iota": np.tile(np.arange(EXPERTS, dtype=f), (P, 1))}


def layouts(i):
    c = np.ascontiguousarray
    f = np.float32

    def tiles(a):
        *lead, k, n = a.shape
        return c(np.moveaxis(a.reshape(*lead, k // P, P, n), -2, 0))

    def cols(a):
        return c(a.reshape(a.shape[0], -1, P, a.shape[2]).transpose(2, 0, 1, 3))

    def strips(w):
        k = w.shape[0]
        o = np.zeros((k, HEADS, HROW), f)
        o[:, :, :HDIM] = w.reshape(k, HEADS, HDIM)
        return o.reshape(k, HEADS * HROW)

    d = dict(shape_constants())
    d["x"] = c(i["x"])
    d["w_in"] = tiles(i["L0_attn_in_proj_w"].transpose(0, 2, 1))
    d["w_xp"] = tiles(i["L0_attn_x_proj_w"].transpose(0, 2, 1))
    d["w_dt"] = c(i["L0_attn_dt_w"].transpose(2, 0, 1))
    d["w_out"] = tiles(i["L0_attn_out_w"].transpose(0, 2, 1))
    d["conv_w"] = c(i["L0_attn_conv_w"])
    d["w_cv"] = cols(i["L0_attn_conv_w"])
    v = np.stack([i["L0_attn_conv_b"], i["L0_attn_dt_b"], i["L0_attn_Dp"]], 1)
    d["vecs"] = c(v.reshape(v.shape[0], 3, -1, P).transpose(3, 0, 1, 2))
    nw = i["L0_attn_norm_w"]
    d["normw"] = c(nw.reshape(nw.shape[0], -1, P).transpose(2, 0, 1))
    d["alog"] = cols(i["L0_attn_A_log"])
    ctx = i["ctx_1024"].transpose(0, 2, 1)
    d["ctxT"] = c(ctx.reshape(ctx.shape[0], -1, P, ctx.shape[2]).transpose(0, 2, 1, 3))
    for n, w in (("w_q", "Wq"), ("w_k", "Wk")):
        d[n] = c(tiles(strips(i["L0_xattn_" + w].T)).reshape(P, -1, HEADS // 4, P))
    d["w_v"] = tiles(strips(i["L0_xattn_Wv"].T))
    bq, bk, bv = (strips(i["L0_xattn_" + n][None])[0] for n in ("bq", "bk", "bv"))
    bk[HDIM::HROW] = 1
    bv[HDIM::HROW] = 1
    d["b_qk"] = c(np.stack([bq, bk]).reshape(2, -1, P).transpose(2, 0, 1))
    d["b_v"] = bv
    d["b_o"] = c(i["L0_xattn_bo"])
    d["w_o"] = tiles(strips(i["L0_xattn_Wo"]).T)
    d["w_g"] = tiles(i["L0_ffn_Wg"])
    d["up"] = c(np.moveaxis(tiles(np.concatenate([i["L0_ffn_Wu"], i["L0_ffn_W1"][None]])), 1, 0))
    d["down"] = c(np.moveaxis(tiles(np.concatenate([i["L0_ffn_Wd"], i["L0_ffn_W2"][None]])), 1, 0))
    d["W1"] = c(i["L0_ffn_W1"])
    return d


UPTO = 3


def kernel(**inputs):
    import concourse.bacc as _bacc
    from concourse import mybir as _mybir
    from concourse.bass_utils import run_bass_kernel_spmd as _run

    nc = _bacc.Bacc("TRN2", target_bir_lowering=False, num_devices=1)
    arrays = layouts({k: np.asarray(v) for k, v in inputs.items()})
    aps = {k: nc.dram_tensor(k + "_dram", a.shape, _mybir.dt.from_np(a.dtype), kind="ExternalInput").ap() for k, a in arrays.items()}
    out = nc.dram_tensor("out_dram", arrays["x"].shape, _mybir.dt.float32, kind="ExternalOutput").ap()
    build(nc, aps, out, UPTO)
    r = _run(nc, [{k + "_dram": a for k, a in arrays.items()}], core_ids=[0])
    return r.results[0]["out_dram"]
```

```python
from contextlib import ExitStack

import numpy as np

import concourse.bass as bass
from concourse import mybir

ALU = mybir.AluOpType
ACT = mybir.ActivationFunctionType
AX = mybir.AxisListType
F32 = mybir.dt.float32
U32 = mybir.dt.uint32
F32R = mybir.dt.float32r

P = 128
BETA = 0.6
EPS = 1e-5
NSTATE = 16
NTAP = 4
QC = P - NSTATE
HEADS, HDIM = 16, 16
HROW = 32
EXPERTS = 8
SP_MAX = 40.0


class Sem:

    def __init__(self, nc, ctx, name):
        self.handle = ctx.enter_context(nc.semaphore(name))
        self.count = 0


class Queue:

    def __init__(self, nc, ctx, name, engine):
        self.engine, self.waited = engine, {}
        self.sem = Sem(nc, ctx, "done_" + name)

    def wait(self, *marks):
        for m in marks:
            if m is None or self.waited.get(m[0], 0) >= m[1]:
                continue
            self.waited[m[0]] = m[1]
            self.engine.wait_ge(m[0].handle, m[1])

    def do(self, f):
        f(self.engine)

    def mark(self, f):
        self.sem.count += 1
        f(self.engine).then_inc(self.sem.handle, 1)
        return (self.sem, self.sem.count)

    def load(self, sem, f):
        sem.count += 16
        f(self.engine).then_inc(sem.handle, 16)
        return (sem, sem.count)

    def last(self):
        return (self.sem, self.sem.count) if self.sem.count else None


def build(nc, d, out, upto=3):
    B, S, D = d["x"].shape
    T = B * S
    NT, TB_, KD = T // P, S // P, D // P
    L = 2
    DI = d["conv_w"].shape[1]
    ET = DI // P
    RANK = 16
    NCH = -(-S // QC)
    CH = [min(QC, S - c * QC) for c in range(NCH)]
    WPAD = NCH * QC + NSTATE
    GN = 4
    F = d["W1"].shape[1]
    FT = F // P

    with ExitStack() as ctx:
        pe, dve, act, pool, sp = (
            Queue(nc, ctx, n, e) for n, e in (("tensor", nc.tensor), ("vector", nc.vector), ("scalar", nc.scalar),
                                              ("gpsimd", nc.gpsimd), ("sync", nc.sync)))
        ALLQ = (pe, dve, act, pool, sp)

        def sb(c, name, shape, dt=F32):
            return c.enter_context(nc.sbuf_tensor(name, shape, dt))

        def sem(name):
            return Sem(nc, ctx, name)

        def load(name, dst, src, *after):
            sp.wait(*after)
            return sp.load(sem("ld_" + name), lambda e: e.dma_start(dst, src))

        def phase_border():
            marks = [q.last() for q in ALLQ]
            for q in ALLQ:
                q.wait(*marks)

        psum = ctx.enter_context(nc.psum_tensor("psum", [P, 8, 512], F32))

        ident = sb(ctx, "ident", [P, P])
        xm = sb(ctx, "xm", [P, NT, D])
        stat = sb(ctx, "stat", [P, NT, 12])
        epst = sb(ctx, "epst", [P, 1])
        x_tok = d["x"].rearrange("b (t p) d -> p (b t) d", p=P)
        out_tok = out.rearrange("b (t p) d -> p (b t) d", p=P)

        ld_ident = load("ident", ident[:], d["ident"])
        ld_x = [load("x0", xm[:, 0:TB_, :], x_tok[:, 0:TB_, :])]
        m_eps = dve.mark(lambda e: e.memset(epst[:], EPS))

        def norm_pieces(lo, hi, src, src_marks):
            dve.wait(*src_marks)
            for t in range(lo, hi):
                m = dve.mark(lambda e, t=t: e.bn_stats(stat[:, t, 0:6], src[:, t, :]))
                if t % TB_ == TB_ - 1:
                    yield
            dve.wait(m)
            for t in range(lo, hi):
                m = dve.mark(lambda e, t=t: e.bn_aggr(stat[:, t, 6:8], stat[:, t, 0:6]))
            act.wait(m, m_eps)
            m = act.mark(lambda e: e.activation(stat[:, lo:hi, 8], stat[:, lo:hi, 7], ACT.Sqrt, bias=epst[:, 0:1]))
            yield
            dve.wait(m)
            m = dve.mark(lambda e: e.reciprocal(stat[:, lo:hi, 9], stat[:, lo:hi, 8]))
            dve.wait(m)
            for t in range(lo, hi):
                m = dve.mark(lambda e, t=t: e.tensor_scalar(xm[:, t, :], src[:, t, :], stat[:, t, 6:7], stat[:, t, 9:10],
                                                            ALU.subtract, ALU.mult))
                if t % TB_ == TB_ - 1 and t < hi - 1:
                    yield
            return m

        def at_once(g):
            while True:
                try:
                    next(g)
                except StopIteration as end:
                    return end.value

        def layernorm(b, src, src_marks):
            return at_once(norm_pieces(b * TB_, (b + 1) * TB_, src, src_marks))

        with ExitStack() as mc:
            w_in = sb(mc, "w_in", [P, L, KD, 2 * DI])
            w_xp = sb(mc, "w_xp", [P, L, ET, RANK + 2 * NSTATE])
            w_dt = sb(mc, "w_dt", [RANK, L, DI])
            w_out = sb(mc, "w_out", [P, L, ET, D])
            w_cv = sb(mc, "w_cv", [P, L, ET, NTAP])
            vecs = sb(mc, "vecs", [P, L, 3, ET])
            normw = sb(mc, "normw", [P, L, KD])
            alog = sb(mc, "alog", [P, L, ET, NSTATE])
            toep = sb(mc, "toep", [P, QC])
            keep = sb(mc, "keep", [P, 1])
            carry_id = sb(mc, "carry_id", [P, NCH, NSTATE])

            square = sb(mc, "square", [P, D])
            xnT = sb(mc, "xnT", [P, KD, S])
            xraw = sb(mc, "xraw", [P, ET, NTAP - 1 + S])
            xs = xraw[:, :, NTAP - 1:NTAP - 1 + D]
            uw = sb(mc, "uw", [P, ET, WPAD])
            xbs = sb(mc, "xbs", [P, 2, ET, WPAD])
            sz = sb(mc, "sz", [P, 2, ET, S])
            delta = sb(mc, "delta", [P, 2, ET, S])
            RBC = RANK + 2 * NSTATE
            dbc = sb(mc, "dbc", [RBC, WPAD])
            uT = sb(mc, "uT", [P, 2, NCH, DI])
            bcol = sb(mc, "bcol", [P, 2, NCH, NSTATE])
            bend = sb(mc, "bend", [P, NCH, NSTATE])
            ccol = sb(mc, "ccol", [P, 2, TB_, NSTATE])
            NG = NSTATE // GN
            filt = sb(mc, "filt", [P, 2, NCH, GN, QC])
            yacc = sb(mc, "yacc", [P, 2, TB_, DI])
            NDA, NH, AHEAD = 5, 9, 3
            dA = sb(mc, "dA", [P, NDA, S])
            hst = sb(mc, "hst", [P, NH, S])

            wt = {}
            wt["normw"] = load("normw", normw[:], d["normw"])
            wt["w_in", 0] = load("w_in0", w_in[:, 0], d["w_in"][:, 0])
            for name, dst in (("w_cv", w_cv), ("vecs", vecs), ("w_xp", w_xp),
                              ("w_dt", w_dt), ("alog", alog), ("toep", toep), ("keep", keep), ("carry_id", carry_id),
                              ("w_out", w_out)):
                wt[name] = load(name, dst[:], d[name])
            ld_x += [load(f"x{b}", xm[:, b * TB_:(b + 1) * TB_, :], x_tok[:, b * TB_:(b + 1) * TB_, :]) for b in range(1, B)]
            wt["w_in", 1] = load("w_in1", w_in[:, 1], d["w_in"][:, 1])

            m_zero = [pool.mark(lambda e: e.memset(xraw[:], 0.0)), pool.mark(lambda e: e.memset(uw[:], 0.0)),
                      pool.mark(lambda e: e.memset(xbs[:], 0.0)), pool.mark(lambda e: e.memset(dbc[:], 0.0))]
            v_free, t_free, x_free = [None] * 3, [None] * 3, [None] * 2
            cnt = {"v": 0, "t": 0, "x": 0, "a": 0, "h": 0}

            def bank(kind, base, free):
                i = cnt[kind] % len(free)
                cnt[kind] += 1
                pe.wait(free[i])
                return i, psum[:, base + i, :]

            def xbank():
                return bank("x", 6, x_free)

            def transpose4(dst, srcs):
                for j, s in enumerate(srcs):
                    f = lambda e, j=j, s=s: e.transpose(dst[:, j * P:(j + 1) * P], s, ident[:])
                    if j < len(srcs) - 1:
                        pe.do(f)
                return pe.mark(f)

            items = [(l, b) for l in range(L) for b in range(B)]
            n_items = len(items)
            stream = [None] * B
            rms = [None] * B

            sq_free = [None]

            def rms_squares(b):
                act.wait(stream[b], m_eps)
                for t in range(b * TB_, (b + 1) * TB_):
                    act.wait(sq_free[0])
                    sq_free[0] = act.mark(lambda e: e.activation(square[:], xm[:, t, :], ACT.Square, accum_out=stat[:, t, 10:11]))

            def rms_root(lo, hi):
                act.wait(sq_free[0])
                return act.mark(lambda e: e.activation(stat[:, lo * TB_:hi * TB_, 11], stat[:, lo * TB_:hi * TB_, 10], ACT.Sqrt,
                                                       scale=1.0 / D, bias=epst[:, 0:1]))

            def rms_inverse(lo, hi, m):
                dve.wait(m)
                m = dve.mark(lambda e: e.reciprocal(stat[:, lo * TB_:hi * TB_, 11], stat[:, lo * TB_:hi * TB_, 11]))
                rms[lo:hi] = [m] * (hi - lo)

            stream[0] = layernorm(0, xm, [ld_x[0]])
            rms_squares(0)
            rms_inverse(0, 1, rms_root(0, 1))

            def other_norms():
                m = yield from norm_pieces(TB_, NT, xm, ld_x[1:])
                stream[1:] = [m] * (B - 1)
                for b in range(1, B):
                    yield
                    rms_squares(b)
                m = rms_root(1, B)
                yield
                rms_inverse(1, B, m)
                yield

            act.wait(wt["alog"])
            m = act.mark(lambda e: e.activation(alog[:], alog[:], ACT.Exp))
            dve.wait(m)
            m_aneg = dve.mark(lambda e: e.tensor_scalar(alog[:], alog[:], -1.0, None, ALU.mult))

            done = [dict() for _ in range(n_items)]
            pe.wait(ld_ident)

            def front(k):
                l, b = items[k]
                par = k % 2
                me, old = done[k], done[k - 2] if k >= 2 else {}
                prev = done[k - 1] if k else {}
                t0 = b * TB_
                dve.wait(stream[b], rms[b], prev.get("xraw_read"), *m_zero)
                for t in range(TB_):
                    m = dve.mark(lambda e: e.tensor_scalar(xs[:, t, :], xm[:, t0 + t, :], stat[:, t0 + t, 11:12],
                                                           None, ALU.mult))
                yield
                pe.wait(m)
                for kt in range(KD):
                    i, bk = xbank()
                    me["xs_read"] = m = transpose4(bk, [xs[:, t, kt * P:(kt + 1) * P] for t in range(TB_)])
                    yield
                    dve.wait(m, prev.get("xnT_read"), wt["normw"])
                    x_free[i] = m_xn = dve.mark(lambda e: e.tensor_scalar(xnT[:, kt, :], bk, normw[:, l, kt:kt + 1],
                                                                          None, ALU.mult))
                yield

                def project(m8):
                    i, bk = xbank()
                    pe.wait(m_xn, wt["w_in", l])
                    for kt in range(KD):
                        f = lambda e: e.matmul(bk, w_in[:, l, kt, m8 * P:(m8 + 1) * P], xnT[:, kt, :],
                                               start=kt == 0, stop=kt == KD - 1)
                        m = pe.mark(f) if kt == KD - 1 else pe.do(f)
                    return i, bk, m

                for m4 in range(ET):
                    i, bk, m = project(m4)
                    yield
                    act.wait(m, me["xs_read"], *m_zero, prev.get("uw_read"), old.get("sz_read"), wt["w_cv"], wt["vecs"])
                    m_raw = act.mark(lambda e: e.copy(xraw[:, m4, NTAP - 1:], bk))
                    dst = uw[:, m4, NSTATE:NSTATE + S]
                    x_free[i] = m = act.mark(lambda e: e.activation(dst, bk, ACT.Identity, scale=w_cv[:, l, m4, NTAP - 1:NTAP],
                                                                       bias=vecs[:, l, 0, m4:m4 + 1]))
                    i, bk, m_z = project(ET + m4)
                    yield
                    for tap in range(NTAP - 1):
                        dve.wait(m)
                        m = dve.mark(lambda e: e.scalar_tensor_tensor(
                            out=dst, in0=xraw[:, m4, tap:tap + S], scalar=w_cv[:, l, m4, tap:tap + 1], in1=dst,
                            op0=ALU.mult, op1=ALU.add))
                    act.wait(m_z)
                    x_free[i] = act.mark(lambda e: e.copy(sz[:, par, m4, :], bk))
                me["conv"] = m
                me["xnT_read"] = pe.last()
                yield
                act.wait(m, old.get("xbs_read"), x_free[i])
                me["xbs"] = m = act.mark(lambda e: e.activation(xbs[:, par, :, NSTATE:NSTATE + S], uw[:, :, NSTATE:NSTATE + S], ACT.Silu))
                me["sz"] = act.mark(lambda e: e.activation(sz[:, par], sz[:, par], ACT.Silu))
                yield
                yield
                i, bk = xbank()
                pe.wait(m, wt["w_xp"])
                for kt in range(ET):
                    f = lambda e: e.matmul(bk[0:RBC, :], w_xp[:, l, kt, :], xbs[:, par, kt, NSTATE:NSTATE + S],
                                           start=kt == 0, stop=kt == ET - 1)
                    m = pe.mark(f) if kt == ET - 1 else pe.do(f)
                yield
                act.wait(m, prev.get("dbc_read"))
                x_free[i] = m_dbc = act.mark(lambda e: e.copy(dbc[:, NSTATE:NSTATE + S], bk[0:RBC, :]))
                yield
                i, bk = xbank()
                pe.wait(m_dbc)
                starts = [c * QC for c in range(NCH)] + [NSTATE + t * P for t in range(TB_)]
                for j, w0 in enumerate(starts):
                    f = lambda e: e.transpose(bk[:, j * RBC:(j + 1) * RBC], dbc[:, w0:w0 + P], ident[0:RBC, 0:RBC])
                    m = pe.mark(f) if j == len(starts) - 1 else pe.do(f)
                yield
                dve.wait(m, wt["keep"], wt["carry_id"], old.get("bcol_read"), old.get("ccol_read"))
                tv = bk[:, 0:len(starts) * RBC].rearrange("p (j r) -> p j r", r=RBC)
                m = dve.mark(lambda e: e.scalar_tensor_tensor(
                    out=bcol[:, par], in0=tv[:, 0:NCH, RANK:RANK + NSTATE], scalar=keep[:, 0:1], in1=carry_id[:],
                    op0=ALU.mult, op1=ALU.add))
                me["bcol"] = m
                x_free[i] = me["ccol"] = dve.mark(lambda e: e.tensor_copy(ccol[:, par], tv[:, NCH:, RANK + NSTATE:]))
                dve.wait(m, wt["toep"], prev.get("bend_read"))
                m_bend = dve.mark(lambda e: e.tensor_scalar(bend[:], bcol[:, par], toep[:, QC - 1:QC], None, ALU.mult))
                for m4 in range(ET):
                    i, bk = xbank()
                    pe.wait(m_dbc, wt["w_dt"])
                    m = pe.mark(lambda e: e.matmul(bk, w_dt[:, l, m4 * P:(m4 + 1) * P], dbc[0:RANK, NSTATE:NSTATE + S], start=True, stop=True))
                    yield
                    act.wait(m, old.get("delta_read"), me["conv"])
                    x_free[i] = m = act.mark(lambda e: e.activation(delta[:, par, m4, :], bk, ACT.Identity, bias=vecs[:, l, 1, m4:m4 + 1]))
                me["dbc_read"] = pe.last()
                yield
                dve.wait(m)
                m = dve.mark(lambda e: e.tensor_scalar(xraw[:, :, NTAP - 1:], delta[:, par], SP_MAX, None, ALU.min))
                yield
                xr = xraw[:, :, NTAP - 1:]
                act.wait(m)
                m2 = act.mark(lambda e: e.activation(xr, xr, ACT.Exp))
                if k + 1 < n_items and items[k + 1][0]:
                    rms_squares(items[k + 1][1])
                yield
                act.wait(m2)
                m2 = act.mark(lambda e: e.activation(xr, xr, ACT.Ln, bias=1.0))
                nb = items[k + 1][1] if k + 1 < n_items and items[k + 1][0] else None
                if nb is not None:
                    m_rms = rms_root(nb, nb + 1)
                yield
                yield
                yield
                if nb is not None:
                    rms_inverse(nb, nb + 1, m_rms)
                for m4 in range(ET):
                    dve.wait(m2)
                    m = dve.mark(lambda e: e.tensor_tensor(delta[:, par, m4, :], delta[:, par, m4, :], xraw[:, m4, NTAP - 1:], ALU.max))
                    pool.wait(m, me["xbs"], *m_zero)
                    m_u = pool.mark(lambda e: e.tensor_tensor(uw[:, m4, NSTATE:NSTATE + S], delta[:, par, m4, :],
                                                              xbs[:, par, m4, NSTATE:NSTATE + S], ALU.mult))
                    yield
                me["delta"] = me["xraw_read"] = m
                yield
                yield
                for c in range(NCH):
                    i, bk = xbank()
                    pe.wait(m_u)
                    m = transpose4(bk, [uw[:, et, c * QC:c * QC + P] for et in range(ET)])
                    yield
                    act.wait(m, old.get("uT_read"))
                    x_free[i] = m_uT = act.mark(lambda e: e.copy(uT[:, par, c, :], bk))
                me["uw_read"] = pe.last()
                for c in range(NCH - 1):
                    yield
                    i, bk = xbank()
                    pe.wait(m_bend, m_uT)
                    m = pe.mark(lambda e: e.matmul(bk[0:NSTATE, :], bend[:, c, :], uT[:, par, c, :], start=True, stop=True))
                    yield
                    act.wait(m, m_uT)
                    x_free[i] = m_uT = act.mark(lambda e: e.copy(uT[0:NSTATE, par, c + 1, :], bk[0:NSTATE, :]))
                me["bend_read"] = pe.last()
                me["uT"] = m_uT

            g_state = {"n": 0}
            filt_free = [None, None]

            def build_filter(k, g):
                slot = g_state["n"] % 2
                g_state["n"] += 1
                pool.wait(done[k]["bcol"], wt["toep"], filt_free[slot])
                par = k % 2
                m = pool.mark(lambda e: e.tensor_tensor(
                    filt[:, slot], toep[:, :].unsqueeze(1).unsqueeze(1).to_broadcast([P, NCH, GN, QC]),
                    bcol[:, par, :, g * GN:(g + 1) * GN].unsqueeze(3).to_broadcast([P, NCH, GN, QC]), ALU.mult))
                done[k]["bcol_read"] = m
                return slot, m

            dA_free, h_free = [None] * NDA, [None] * NH
            y_free = [None, None]
            ready_filter = {}

            def add_state(k, n, hs, t):
                par, me = k % 2, done[k]
                i, bk = bank("t", 3, t_free)
                pe.wait(hs[-1][1])
                m = transpose4(bk, [hst[:, s, t * P:(t + 1) * P] for s, _ in hs])
                c = ccol[:, par, t, n:n + 1]
                if n == 0:
                    dve.wait(m, y_free[par], me["ccol"])
                    f = lambda e: e.tensor_scalar(yacc[:, par, t, :], bk, c, None, ALU.mult)
                else:
                    dve.wait(m, me["y", t])
                    f = lambda e: e.scalar_tensor_tensor(out=yacc[:, par, t, :], in0=bk, scalar=c, in1=yacc[:, par, t, :],
                                                         op0=ALU.mult, op1=ALU.add)
                me["y", t] = t_free[i] = dve.mark(f)
                if t == TB_ - 1:
                    for s, _ in hs:
                        h_free[s] = pe.last()
                    if n == NSTATE - 1:
                        me["ccol_read"] = t_free[i]

            decayed = []

            def run_ahead():
                while len(decayed) <= AHEAD and cnt["a"] < n_items * NSTATE * ET:
                    k, n, et = cnt["a"] // (NSTATE * ET), cnt["a"] // ET % NSTATE, cnt["a"] % ET
                    me, l = done[k], items[k][0]
                    if "delta" not in me:
                        break
                    a = cnt["a"] % NDA
                    cnt["a"] += 1
                    act.wait(dA_free[a], me["delta"], m_aneg)
                    m = act.mark(lambda e: e.activation(dA[:, a, :], delta[:, k % 2, et, :], ACT.Exp, scale=alog[:, l, et, n:n + 1]))
                    decayed.append((a, m))
                    if (n, et) == (NSTATE - 1, ET - 1):
                        me["delta_read"] = m

            def main(k, pend, side):
                l, b = items[k]
                par = k % 2
                me = done[k]
                for n in range(NSTATE):
                    g = n // GN
                    slot, m_f = ready_filter[k, g]
                    if n % GN == 0 and g + 1 < NG:
                        ready_filter[k, g + 1] = build_filter(k, g + 1)
                    if g == NG - 1 and k + 1 < n_items and (k + 1, 0) not in ready_filter and "bcol" in done[k + 1]:
                        ready_filter[k + 1, 0] = build_filter(k + 1, 0)
                    hs = []
                    for et in range(ET):
                        i, bk = bank("v", 0, v_free)
                        pe.wait(m_f, me["uT"])
                        for c in range(NCH):
                            f = lambda e: e.matmul(bk[:, c * QC:c * QC + CH[c]], uT[:, par, c, et * P:(et + 1) * P],
                                                   filt[:, slot, c, n % GN, 0:CH[c]], start=True, stop=True)
                            m_v = pe.mark(f) if c == NCH - 1 else pe.do(f)
                        run_ahead()
                        a, m_a = decayed.pop(0)
                        s = cnt["h"] % NH
                        cnt["h"] += 1
                        dve.wait(m_v, m_a, h_free[s])
                        m_h = dve.mark(lambda e: e.tensor_tensor_scan(hst[:, s, :], dA[:, a, :], bk, 0.0, ALU.mult, ALU.add))
                        v_free[i] = dA_free[a] = m_h
                        hs.append((s, m_h))
                        if pend is not None:
                            add_state(*pend, et)
                        next(side, None)
                    if n % GN == GN - 1:
                        filt_free[slot] = pe.last()
                    pend = (k, n, hs)
                me["uT_read"] = pe.last()
                import os
                if os.environ.get("PIECES"):
                    print("left", k, sum(1 for _ in side))
                for _ in side:
                    pass
                if k + 1 < n_items and (k + 1, 0) not in ready_filter:
                    ready_filter[k + 1, 0] = build_filter(k + 1, 0)
                return pend

            def back(k):
                l, b = items[k]
                par = k % 2
                me = done[k]
                for et in range(ET):
                    i, bk = xbank()
                    pe.wait(*[me["y", t] for t in range(TB_)])
                    m = transpose4(bk, [yacc[:, par, t, et * P:(et + 1) * P] for t in range(TB_)])
                    yield
                    dve.wait(m, me["xbs"])
                    xd = xbs[:, par, et, NSTATE:NSTATE + S]
                    x_free[i] = m = dve.mark(lambda e: e.scalar_tensor_tensor(
                        out=xd, in0=xd, scalar=vecs[:, l, 2, et:et + 1], in1=bk, op0=ALU.mult, op1=ALU.add))
                    pool.wait(m, me["sz"])
                    m_g = pool.mark(lambda e: e.tensor_tensor(sz[:, par, et, :], sz[:, par, et, :], xd, ALU.mult))
                y_free[par] = pe.last()
                me["xbs_read"] = m_g
                yield
                yield
                for t in range(TB_):
                    i, bk = xbank()
                    pe.wait(m_g, wt["w_out"])
                    for kt in range(ET):
                        f = lambda e: e.matmul(bk[:, 0:D], sz[:, par, kt, t * P:(t + 1) * P], w_out[:, l, kt, :],
                                               start=kt == 0, stop=kt == ET - 1)
                        m = pe.mark(f) if kt == ET - 1 else pe.do(f)
                    yield
                    dve.wait(m)
                    x_free[i] = dve.mark(lambda e: e.tensor_tensor(xm[:, b * TB_ + t, :], xm[:, b * TB_ + t, :], bk[:, 0:D], ALU.add))
                me["sz_read"] = pe.last()
                stream[b] = dve.last()

            def sides(k):
                for _ in range(ET):
                    yield
                if k:
                    yield from back(k - 1)
                else:
                    yield from other_norms()
                if k + 1 < n_items:
                    yield from front(k + 1)

            at_once(front(0))
            ready_filter[0, 0] = build_filter(0, 0)
            pend = None
            for k in range(n_items):
                pend = main(k, pend, sides(k))
            for t in range(TB_):
                add_state(*pend, t)
            for _ in back(n_items - 1):
                pass
        phase_border()

        xres = sb(ctx, "xres", [P, NT, D])
        m_x1 = []
        for b in range(B):
            r = xres[:, b * TB_:(b + 1) * TB_, :]
            dve.wait(load(f"xres{b}", r, x_tok[:, b * TB_:(b + 1) * TB_, :]))
            m_x1.append(dve.mark(lambda e: e.tensor_tensor(r, r, xm[:, b * TB_:(b + 1) * TB_, :], ALU.add)))

        if upto >= 2:
            with ExitStack() as ac:
                HG = HEADS // 4
                UH = HEADS // 2
                UG = UH // 4
                w_q = sb(ac, "w_q", [P, KD, HG, P])
                w_k = sb(ac, "w_k", [P, KD, HG, P])
                w_v = sb(ac, "w_v", [P, KD, HEADS * HROW])
                w_o = sb(ac, "w_o", [P, HG, D])
                b_qk = sb(ac, "b_qk", [P, 2, HG])
                b_v = sb(ac, "b_v", [P, HEADS * HROW])
                b_o = sb(ac, "b_o", [P, D])
                ctxT = sb(ac, "ctxT", [P, 2, KD, S])
                xnT = sb(ac, "axnT", [P, KD, S])
                flat = sb(ac, "flat", [P, 2, S])
                part = sb(ac, "part", [P, 2, 2, UG, S], F32R)
                qk = sb(ac, "qk", [P, 2, 2, UH, S], F32R)
                vt = sb(ac, "vt", [P, 2, TB_, HEADS * HROW])
                nmax = sb(ac, "nmax", [P, 2, TB_, UH])
                nsplit = sb(ac, "nsplit", [P, 2, TB_, 2 * UH], F32R)
                nrow = sb(ac, "nrow", [2 * UH, 2, S], F32R)
                NPT = 2
                pT = sb(ac, "pT", [P, NPT, 4, S])
                oT = sb(ac, "oT", [P, HG, S])
                rc = sb(ac, "rc", [P, 4 * TB_])
                otok = sb(ac, "otok", [P, S])
                aw = {n: load(n, t[:], d[n]) for n, t in (("w_q", w_q), ("w_k", w_k), ("w_v", w_v), ("w_o", w_o),
                      ("b_qk", b_qk))}
                aw["b_v"] = load("b_v", b_v[:], d["b_v"].partition_broadcast(P))
                aw["b_o"] = load("b_o", b_o[:], d["b_o"].partition_broadcast(P))
                ld_ctx = [load(f"ctx{b}", ctxT[:, b], d["ctxT"][b]) for b in range(2)]
                s_strip = [[sem(f"strips_{o}{i}") for i in range(2)] for o in ("sync", "gpsimd")]
                s_rows = [sem("rows0"), sem("rows1")]
                NPAIR, PV, ONE0, NONE = 2, 4, 5, 3
                pair_free, pv_free, one_free = [None] * NPAIR, [None], [None] * NONE
                pc = {"n": 0, "p": 0, "f": 0, "o": 0}
                pT_free, flat_free = [None] * NPT, [None, None]
                ctx_read, vt_read, oT_read, xnT_read, rc_read = [None, None], [None, None], [None], [None], [None]
                ud = [dict() for _ in range(2 * B)]
                m_v, m_x2, m_div = [None] * B, [None] * B, {}

                def one(f_list):
                    i = pc["o"] % NONE
                    pc["o"] += 1
                    bk = psum[:, ONE0 + i, :]
                    pe.wait(one_free[i])
                    for f in f_list[:-1]:
                        pe.do(lambda e: f(e, bk))
                    return i, bk, pe.mark(lambda e: f_list[-1](e, bk))

                def prepare(u):
                    b, half = divmod(u, 2)
                    cp, par, me = b % 2, u % 2, ud[u]
                    prev, old = (ud[u - 1] if u else {}), (ud[u - 2] if u > 1 else {})
                    if half == 0:
                        ln = layernorm(b, xres, [m_x1[b]])
                        yield
                        yield
                        for kt in range(KD):
                            pe.wait(ln)
                            i, bk, m = one([lambda e, bk, t=t: e.transpose(bk[:, t * P:(t + 1) * P], xm[:, b * TB_ + t, kt * P:(kt + 1) * P], ident[:])
                                     for t in range(TB_)])
                            yield
                            dve.wait(m, xnT_read[0])
                            one_free[i] = me["xn"] = dve.mark(lambda e: e.tensor_copy(xnT[:, kt, :], bk))
                    else:
                        me["xn"] = prev["xn"]
                    for g in range(UG):
                        for which, w, src, ready in ((1, w_k, ctxT[:, cp], ld_ctx[b]), (0, w_q, xnT, me["xn"])):
                            hg = half * UG + g
                            pe.wait(aw["w_k"], aw["w_q"], ready)
                            i, bk, m = one([lambda e, bk, kt=kt: e.matmul(bk, w[:, kt, hg, :], src[:, kt, :], start=kt == 0, stop=kt == KD - 1)
                                     for kt in range(KD)])
                            yield
                            z = pc["f"] % 2
                            pc["f"] += 1
                            act.wait(m, aw["b_qk"], flat_free[z])
                            one_free[i] = m = act.mark(lambda e: e.activation(flat[:, z, :], bk, ACT.Identity, bias=b_qk[:, which, hg:hg + 1]))
                            dve.wait(m, prev.get(("strips", 0)), prev.get(("strips", 1)))
                            hi, lo = part[:, which, 0, g, :], part[:, which, 1, g, :]
                            m = dve.mark(lambda e: e.tensor_copy(hi, flat[:, z, :]))
                            dve.wait(m)
                            flat_free[z] = m = dve.mark(lambda e: e.tensor_tensor(lo, flat[:, z, :], hi.bitcast(F32), ALU.subtract))
                    if half:
                        xnT_read[0] = pe.last()
                    me["parts"] = m
                    yield
                    if half == 0:
                        for kv in range(TB_):
                            pe.wait(aw["w_v"], ld_ctx[b])
                            i, bk, m = one([lambda e, bk, kt=kt: e.matmul(bk, ctxT[:, cp, kt, kv * P:(kv + 1) * P], w_v[:, kt, :],
                                                               start=kt == 0, stop=kt == KD - 1) for kt in range(KD)])
                            yield
                            dve.wait(m, aw["b_v"], vt_read[cp])
                            one_free[i] = m_v[b] = dve.mark(lambda e: e.tensor_tensor(vt[:, cp, kv, :], bk, b_v[:], ALU.add))
                    else:
                        ctx_read[cp] = pe.last()
                        if b + 2 < B:
                            ld_ctx.append(load(f"ctx{b + 2}", ctxT[:, cp], d["ctxT"][b + 2], ctx_read[cp]))

                def strips(u):
                    par, me = u % 2, ud[u]
                    for queue in (sp, pool):
                        queue.wait(me["parts"], ud[u - 2]["qk_read"] if u > 1 else None)
                    n = 0
                    for strip, parts in enumerate(zip((0, 0, 1, 1), (0, 1, 0, 1))):
                        for which, p in enumerate(parts):
                            dst = qk[strip * HROW:(strip + 1) * HROW, par, which].rearrange("r (i g) t -> r i (g t)", i=4)
                            for i in range(4):
                                src = part[i * HROW:(i + 1) * HROW, which, p].rearrange("r g t -> r (g t)")
                                z = n % 8 in (1, 4, 6)
                                n += 1
                                m = (sp, pool)[z].load(s_strip[z][par], lambda e: e.dma_start(dst[:, i].bitcast(F32), src.bitcast(F32)))
                                me["strips", z] = m

                def pair(mms):
                    i = pc["n"] % NPAIR
                    pc["n"] += 1
                    pe.wait(pair_free[i])
                    pe.do(lambda e: mms[0](e, psum[:, 2 * i, :]))
                    return i, pe.mark(lambda e: mms[1](e, psum[:, 2 * i + 1, :]))

                def maxima(u):
                    par, me = u % 2, ud[u]
                    old = ud[u - 2] if u > 1 else {}
                    q, k = qk[:, par, 0], qk[:, par, 1]
                    for h in range(0, UH, 2):
                        for t in range(TB_):
                            pe.wait(me["strips", 0], me["strips", 1])
                            i, m = pair([lambda e, o, h=h + j: e.matmul(o, q[:, h, t * P:(t + 1) * P], k[:, h, :], start=True, stop=True)
                                         for j in range(2)])
                            dve.wait(m, old.get("nmax_read"))
                            pair_free[i] = m = dve.mark(lambda e: e.tensor_reduce(nmax[:, par, t, h:h + 2], psum[:, 2 * i:2 * i + 2, :], AX.X,
                                                                                  ALU.max, negate=True))
                            yield
                    dve.wait(m, old.get("nsplit_read"))
                    m = dve.mark(lambda e: e.tensor_copy(nsplit[:, par, :, 0:UH], nmax[:, par]))
                    dve.wait(m)
                    m = dve.mark(lambda e: e.tensor_tensor(nsplit[:, par, :, UH:], nmax[:, par], nsplit[:, par, :, 0:UH].bitcast(F32), ALU.subtract))
                    me["nmax_read"] = m
                    yield
                    pe.wait(m, ld_ident)
                    i, bk, m = one([lambda e, bk, t=t: e.transpose(bk[0:2 * UH, t * P:(t + 1) * P], nsplit[:, par, t, :].bitcast(F32), ident[:])
                             for t in range(TB_)])
                    me["nsplit_read"] = m
                    yield
                    dve.wait(m, old.get("rows"))
                    one_free[i] = m = dve.mark(lambda e: e.tensor_copy(nrow[:, par, :], bk[0:2 * UH, :]))
                    sp.wait(m)
                    for p in range(2):
                        r = 2 * p * HROW + HDIM
                        me["rows"] = sp.load(s_rows[par], lambda e: e.dma_start(qk[r:r + 1, par, 0, :, :].bitcast(F32),
                                                                         nrow[p * UH:(p + 1) * UH, par, :].bitcast(F32)))

                def weighted(u, side, row_side):
                    b, half = divmod(u, 2)
                    par, cp, me = u % 2, b % 2, ud[u]
                    q, k = qk[:, par, 0], qk[:, par, 1]

                    def values(g, kv, z, m_e):
                        hg = half * UG + g
                        pe.wait(m_e, m_v[b], pv_free[0])
                        for i in range(4):
                            c0 = (hg * 4 + i) * HROW
                            f = lambda e: e.matmul(psum[i * HROW:(i + 1) * HROW, PV, :], vt[:, cp, kv, c0:c0 + HROW], pT[:, z, i, :],
                                                   start=kv == 0, stop=kv == TB_ - 1, tile_position=(0, i * HROW))
                            m = pe.mark(f) if i == 3 else pe.do(f)
                        pT_free[z] = m
                        if kv == TB_ - 1:
                            act.wait(m, oT_read[0])
                            pv_free[0] = m_div[hg] = act.mark(lambda e: e.copy(oT[:, hg, :], psum[:, PV, :]))

                    def divide(g):
                        hg = half * UG + g
                        pe.wait(m_div[hg])
                        i, bk, m = one([lambda e, bk, t=t: e.transpose(bk[:, t * P:(t + 1) * P], oT[:, hg, t * P:(t + 1) * P], ident[:]) for t in range(TB_)])
                        yield
                        v = bk.rearrange("p (n r) -> p n r", r=HROW)
                        dve.wait(m)
                        m = dve.mark(lambda e: e.reciprocal(rc[:], v[:, :, HDIM]))
                        dve.wait(m, rc_read[0])
                        one_free[i] = m = dve.mark(lambda e: e.tensor_tensor(otok[:].rearrange("p (n r) -> p n r", r=HROW), v,
                                                                             rc[:].unsqueeze(2).to_broadcast([P, 4 * TB_, HROW]), ALU.mult))
                        yield
                        pe.wait(m)
                        i, bk, m = one([lambda e, bk, t=t: e.transpose(bk[:, t * P:(t + 1) * P], otok[:, t * P:(t + 1) * P], ident[:]) for t in range(TB_)])
                        rc_read[0] = m
                        yield
                        act.wait(m)
                        one_free[i] = m_div[hg] = act.mark(lambda e: e.copy(oT[:, hg, :], bk))

                    before = None
                    for g in range(UG):
                        for kv in range(TB_):
                            z = pc["p"] % NPT
                            pc["p"] += 1
                            for hp in range(2):
                                pe.wait(me["rows"])
                                i, m = pair([lambda e, o, h=(2 * hp + j) * UG + g: e.matmul(o, k[:, h, kv * P:(kv + 1) * P], q[:, h, :], start=True, stop=True)
                                             for j in range(2)])
                                act.wait(m, pT_free[z])
                                pair_free[i] = m_e = act.mark(lambda e: e.activation(pT[:, z, 2 * hp:2 * hp + 2], psum[:, 2 * i:2 * i + 2, :], ACT.Exp,
                                                                                     scale=HDIM ** -0.5))
                                slot = (g * TB_ + kv) * 2 + hp
                                for j in range(2):
                                    if slot >= ROWS_FROM:
                                        next(row_side, None)
                                    next(side, None)
                            if before is not None:
                                values(*before)
                                if before[1] == TB_ - 1:
                                    rest.append(divide(before[0]))
                            before = (g, kv, z, m_e)
                    me["qk_read"] = pe.last()
                    values(*before)
                    rest.append(divide(UG - 1))
                    if half:
                        vt_read[cp] = pe.last()
                        rest.append(project_out(b))

                def project_out(b):
                    for t in range(TB_):
                        if t:
                            yield
                        pe.wait(aw["w_o"], *m_div.values())
                        i, bk, m = one([lambda e, bk, hg=hg: e.matmul(bk[:, 0:D], oT[:, hg, t * P:(t + 1) * P], w_o[:, hg, :], start=hg == 0, stop=hg == HG - 1)
                                 for hg in range(HG)])
                        dve.wait(m, aw["b_o"])
                        r = xres[:, b * TB_ + t, :]
                        one_free[i] = m = dve.mark(lambda e: e.tensor_tensor(r, r, bk[:, 0:D], ALU.add))
                        dve.wait(m)
                        m_x2[b] = dve.mark(lambda e: e.tensor_tensor(r, r, b_o[:], ALU.add))
                    oT_read[0] = pe.last()

                def alternate(*parts):
                    parts = list(parts)
                    while parts:
                        for g in list(parts):
                            if next(g, g) is g:
                                parts.remove(g)
                            else:
                                yield

                NU = 2 * B
                rest = []

                def leftovers():
                    while rest:
                        yield from rest.pop(0)

                ROWS_FROM = 4

                def sides(u):
                    yield from alternate(leftovers(), prepare(u + 2) if u + 2 < NU else iter(()))
                    yield from leftovers()

                for _ in prepare(0):
                    pass
                strips(0)
                for _ in prepare(1):
                    pass
                strips(1)
                for _ in maxima(0):
                    pass
                for u in range(NU):
                    side, rows = sides(u), maxima(u + 1) if u + 1 < NU else iter(())
                    weighted(u, side, rows)
                    for _ in alternate(rows, side):
                        pass
                    if u + 2 < NU:
                        strips(u + 2)
                for _ in leftovers():
                    pass
            phase_border()

        if upto >= 3:
            with ExitStack() as fc:
                w_g = sb(fc, "w_g", [P, KD, EXPERTS])
                raw = sb(fc, "raw", [P, 2, 2, KD * F])
                wh = sb(fc, "wh", [P, 2, 2, KD * F], F32R)
                wl = sb(fc, "wl", [P, 2, 2, KD * F], F32R)
                xn = sb(fc, "xn", [P, 2, KD, S])
                xh = sb(fc, "xh", [P, B, KD, S], F32R)
                xl = sb(fc, "xl", [P, B, KD, S], F32R)
                NHB = 2
                h32 = sb(fc, "h32", [P, NHB, FT, S])
                hh = sb(fc, "hh", [P, NHB, FT, S], F32R)
                hl = sb(fc, "hl", [P, NHB, FT, S], F32R)
                gate = sb(fc, "gate", [P, NT, 48])
                gidx = sb(fc, "gidx", [P, NT, 8], U32)
                iota = sb(fc, "iota", [P, EXPERTS])
                order = [EXPERTS] + list(range(EXPERTS))
                raw_ld, raw_read, w_ready, w_read = {}, [None, None], {}, [None, None]

                def load_expert(j):
                    x, z = order[j], j % 2
                    raw_ld[j] = [load(f"up{x}", raw[:, z, 0].rearrange("p (k f) -> p k f", k=KD), d["up"][x], raw_read[z]),
                                 load(f"down{x}", raw[:, z, 1].rearrange("p (k f) -> p k f", k=FT), d["down"][x], raw_read[z])]

                def split_expert(j):
                    z = j % 2
                    pool.wait(*raw_ld[j], w_read[z])
                    for half in range(2):
                        m = pool.mark(lambda e: e.tensor_copy(wh[:, z, half], raw[:, z, half]))
                        pool.wait(m)
                        m = pool.mark(lambda e: e.tensor_tensor(wl[:, z, half], raw[:, z, half], wh[:, z, half].bitcast(F32), ALU.subtract))
                    w_ready[j] = raw_read[z] = m

                ld_wg = load("w_g", w_g[:], d["w_g"])
                ld_iota = load("iota", iota[:], d["iota"])
                load_expert(0)
                load_expert(1)
                split_expert(0)

                hid_free, out_free, tr_free = [None] * 4, [None] * 3, [None]
                c3 = {"h": 0, "o": 0}
                h_free = [None] * NHB
                xn_read = [None, None]
                m_x, m_cw = [None] * B, [None] * B
                m_res = [None] * NT

                def normalise(b):
                    par = b % 2
                    ln = layernorm(b, xres, [m_x2[b]])
                    for kt in range(KD):
                        pe.wait(ln, tr_free[0])
                        for t in range(TB_):
                            f = lambda e: e.transpose(psum[:, 7, t * P:(t + 1) * P], xm[:, b * TB_ + t, kt * P:(kt + 1) * P], ident[:])
                            m = pe.mark(f) if t == TB_ - 1 else pe.do(f)
                        act.wait(m, xn_read[par])
                        tr_free[0] = m = act.mark(lambda e: e.copy(xn[:, par, kt, :], psum[:, 7, :]))
                        dve.wait(m)
                        m = dve.mark(lambda e: e.tensor_copy(xh[:, b, kt, :], xn[:, par, kt, :]))
                        dve.wait(m)
                        m_x[b] = dve.mark(lambda e: e.tensor_tensor(xl[:, b, kt, :], xn[:, par, kt, :], xh[:, b, kt, :].bitcast(F32), ALU.subtract))

                def route(b):
                    par = b % 2
                    lo, hi = b * TB_, (b + 1) * TB_
                    pe.wait(m_x[b], ld_wg, tr_free[0])
                    for t in range(TB_):
                        for kt in range(KD):
                            f = lambda e: e.matmul(psum[:, 7, t * EXPERTS:(t + 1) * EXPERTS],
                                                   xn[:, par, kt, t * P:(t + 1) * P], w_g[:, kt, :],
                                                   start=kt == 0, stop=kt == KD - 1)
                            m = pe.mark(f) if (t, kt) == (TB_ - 1, KD - 1) else pe.do(f)
                    xn_read[par] = m
                    lg = psum[:, 7, 0:TB_ * EXPERTS].rearrange("p (t x) -> p t x", x=EXPERTS)
                    G = gate[:, lo:hi, :]
                    bc = lambda c: G[:, :, c:c + 1].to_broadcast([P, TB_, EXPERTS])
                    dve.wait(m, ld_iota)
                    m = dve.mark(lambda e: e.tensor_reduce(G[:, :, 40], lg, AX.X, ALU.max))
                    dve.wait(m)
                    tr_free[0] = m = dve.mark(lambda e: e.tensor_tensor(G[:, :, 0:8], lg, bc(40), ALU.subtract))
                    act.wait(m)
                    m = act.mark(lambda e: e.activation(G[:, :, 0:8], G[:, :, 0:8], ACT.Exp))
                    dve.wait(m)
                    m = dve.mark(lambda e: e.tensor_reduce(G[:, :, 41], G[:, :, 0:8], AX.X, ALU.add))
                    dve.wait(m)
                    m = dve.mark(lambda e: e.reciprocal(G[:, :, 42], G[:, :, 41]))
                    dve.wait(m)
                    m = dve.mark(lambda e: e.tensor_tensor(G[:, :, 0:8], G[:, :, 0:8], bc(42), ALU.mult))
                    dve.wait(m)
                    for t in range(lo, hi):
                        m = dve.mark(lambda e: e.max(gate[:, t, 8:16], gate[:, t, 0:8]))
                    dve.wait(m)
                    for t in range(lo, hi):
                        m = dve.mark(lambda e: e.max_index(gidx[:, t, :], gate[:, t, 8:16], gate[:, t, 0:8]))
                    m2 = dve.mark(lambda e: e.tensor_tensor(G[:, :, 43], G[:, :, 8], G[:, :, 9], ALU.add))
                    dve.wait(m, m2)
                    m = dve.mark(lambda e: e.reciprocal(G[:, :, 44], G[:, :, 43]))
                    m2 = dve.mark(lambda e: e.tensor_copy(G[:, :, 46:48], gidx[:, lo:hi, 0:2]))
                    dve.wait(m, m2)
                    m = dve.mark(lambda e: e.tensor_tensor(G[:, :, 16:18], G[:, :, 8:10], G[:, :, 44:45].to_broadcast([P, TB_, 2]), ALU.mult))
                    dve.wait(m)
                    for t in range(lo, hi):
                        for j in range(2):
                            m = dve.mark(lambda e: e.tensor_scalar(gate[:, t, 24 + 8 * j:32 + 8 * j], iota[:],
                                                                   gate[:, t, 46 + j:47 + j], gate[:, t, 16 + j:17 + j],
                                                                   ALU.is_equal, ALU.mult))
                    dve.wait(m)
                    m_cw[b] = dve.mark(lambda e: e.tensor_tensor(G[:, :, 24:32], G[:, :, 24:32], G[:, :, 32:40], ALU.add))

                def three(dst, ah, al, bh, bl, first, last):
                    for n, (p, q) in enumerate(((ah, bh), (al, bh), (ah, bl))):
                        f = lambda e: e.matmul(dst, p, q, start=first and n == 0, stop=last and n == 2)
                        m = pe.mark(f) if last and n == 2 else pe.do(f)
                    return m

                def hidden(j, b, hz):
                    z = j % 2
                    pe.wait(w_ready[j], m_x[b])
                    for ft in range(FT):
                        i = c3["h"] % 4
                        c3["h"] += 1
                        pe.wait(hid_free[i])
                        for kt in range(KD):
                            w0 = kt * F + ft * P
                            m = three(psum[:, i, :], wh[:, z, 0, w0:w0 + P], wl[:, z, 0, w0:w0 + P], xh[:, b, kt, :], xl[:, b, kt, :],
                                      kt == 0, kt == KD - 1)
                        act.wait(m, h_free[hz])
                        hid_free[i] = m = act.mark(lambda e: e.activation(h32[:, hz, ft, :], psum[:, i, :], ACT.Gelu))
                        dve.wait(m, h_free[hz])
                        m = dve.mark(lambda e: e.tensor_copy(hh[:, hz, ft, :], h32[:, hz, ft, :]))
                        dve.wait(m)
                        m = dve.mark(lambda e: e.tensor_tensor(hl[:, hz, ft, :], h32[:, hz, ft, :], hh[:, hz, ft, :].bitcast(F32), ALU.subtract))
                    return m

                def outputs(j, b, hz, m_h):
                    x, z = order[j], j % 2
                    pe.wait(m_h)
                    for t in range(TB_):
                        i = c3["o"] % 3
                        c3["o"] += 1
                        pe.wait(out_free[i])
                        for ft in range(FT):
                            w0 = ft * D
                            m = three(psum[:, 4 + i, 0:D], hh[:, hz, ft, t * P:(t + 1) * P], hl[:, hz, ft, t * P:(t + 1) * P],
                                      wh[:, z, 1, w0:w0 + D], wl[:, z, 1, w0:w0 + D], ft == 0, ft == FT - 1)
                        tt = b * TB_ + t
                        r = xres[:, tt, :]
                        if x == EXPERTS:
                            dve.wait(m)
                            g = lambda e: e.tensor_tensor(r, r, psum[:, 4 + i, 0:D], ALU.add)
                        else:
                            dve.wait(m, m_res[tt], m_cw[b])
                            g = lambda e: e.scalar_tensor_tensor(out=r, in0=psum[:, 4 + i, 0:D], scalar=gate[:, tt, 24 + x:25 + x],
                                                                 in1=r, op0=ALU.mult, op1=ALU.add)
                        m_res[tt] = out_free[i] = dve.mark(g)
                    h_free[hz] = pe.last()

                stored = []
                normalise(0)
                steps = [(j, b) for j in range(len(order)) for b in range(B)]
                before = None
                for n, (j, b) in enumerate(steps):
                    if b == 1 and j + 1 < len(order):
                        split_expert(j + 1)
                    if j == 0 and b + 1 < B:
                        normalise(b + 1)
                    m_h = hidden(j, b, n % NHB)
                    if b == 1 and j + 2 < len(order):
                        load_expert(j + 2)
                    if j == 0:
                        route(b)
                    if before is not None:
                        outputs(*before)
                        if before[1] == B - 1:
                            w_read[before[0] % 2] = pe.last()
                    before = (j, b, n % NHB, m_h)
                outputs(*before)

        s_out = sem("stored")
        for b in range(B):
            sp.wait(m_res[(b + 1) * TB_ - 1] if upto >= 3 else dve.last())
            m = sp.load(s_out, lambda e, b=b: e.dma_start(out_tok[:, b * TB_:(b + 1) * TB_, :], xres[:, b * TB_:(b + 1) * TB_, :]))
        sp.wait(m)


def shape_constants():
    f = np.float32
    toep = np.zeros((P, QC), np.float64)
    toep[:NSTATE] = BETA ** (np.arange(QC) + 1)
    for s in range(QC):
        toep[NSTATE + s, s:] = BETA ** np.arange(QC - s)
    keep = (np.arange(P) >= NSTATE).astype(f)[:, None]
    n_chunks = -(-512 // QC)
    carry_id = np.zeros((P, n_chunks, NSTATE), f)
    carry_id[:NSTATE] = np.eye(NSTATE, dtype=f)[:, None, :]
    return {"toep": toep.astype(f), "keep": keep, "carry_id": carry_id, 
            "ident": np.eye(P, dtype=f), "iota": np.tile(np.arange(EXPERTS, dtype=f), (P, 1))}


def layouts(i):
    c = np.ascontiguousarray
    f = np.float32

    def tiles(a):
        *lead, k, n = a.shape
        return c(np.moveaxis(a.reshape(*lead, k // P, P, n), -2, 0))

    def cols(a):
        return c(a.reshape(a.shape[0], -1, P, a.shape[2]).transpose(2, 0, 1, 3))

    def strips(w):
        k = w.shape[0]
        o = np.zeros((k, HEADS, HROW), f)
        o[:, :, :HDIM] = w.reshape(k, HEADS, HDIM)
        return o.reshape(k, HEADS * HROW)

    d = dict(shape_constants())
    d["x"] = c(i["x"])
    d["w_in"] = tiles(i["L0_attn_in_proj_w"].transpose(0, 2, 1))
    d["w_xp"] = tiles(i["L0_attn_x_proj_w"].transpose(0, 2, 1))
    d["w_dt"] = c(i["L0_attn_dt_w"].transpose(2, 0, 1))
    d["w_out"] = tiles(i["L0_attn_out_w"].transpose(0, 2, 1))
    d["conv_w"] = c(i["L0_attn_conv_w"])
    d["w_cv"] = cols(i["L0_attn_conv_w"])
    v = np.stack([i["L0_attn_conv_b"], i["L0_attn_dt_b"], i["L0_attn_Dp"]], 1)
    d["vecs"] = c(v.reshape(v.shape[0], 3, -1, P).transpose(3, 0, 1, 2))
    nw = i["L0_attn_norm_w"]
    d["normw"] = c(nw.reshape(nw.shape[0], -1, P).transpose(2, 0, 1))
    d["alog"] = cols(i["L0_attn_A_log"])
    ctx = i["ctx_1024"].transpose(0, 2, 1)
    d["ctxT"] = c(ctx.reshape(ctx.shape[0], -1, P, ctx.shape[2]).transpose(0, 2, 1, 3))
    for n, w in (("w_q", "Wq"), ("w_k", "Wk")):
        d[n] = c(tiles(strips(i["L0_xattn_" + w].T)).reshape(P, -1, HEADS // 4, P))
    d["w_v"] = tiles(strips(i["L0_xattn_Wv"].T))
    bq, bk, bv = (strips(i["L0_xattn_" + n][None])[0] for n in ("bq", "bk", "bv"))
    bk[HDIM::HROW] = 1
    bv[HDIM::HROW] = 1
    d["b_qk"] = c(np.stack([bq, bk]).reshape(2, -1, P).transpose(2, 0, 1))
    d["b_v"] = bv
    d["b_o"] = c(i["L0_xattn_bo"])
    d["w_o"] = tiles(strips(i["L0_xattn_Wo"]).T)
    d["w_g"] = tiles(i["L0_ffn_Wg"])
    d["up"] = c(np.moveaxis(tiles(np.concatenate([i["L0_ffn_Wu"], i["L0_ffn_W1"][None]])), 1, 0))
    d["down"] = c(np.moveaxis(tiles(np.concatenate([i["L0_ffn_Wd"], i["L0_ffn_W2"][None]])), 1, 0))
    d["W1"] = c(i["L0_ffn_W1"])
    return d


UPTO = 3


def kernel(**inputs):
    import concourse.bacc as _bacc
    from concourse import mybir as _mybir
    from concourse.bass_utils import run_bass_kernel_spmd as _run

    nc = _bacc.Bacc("TRN2", target_bir_lowering=False, num_devices=1)
    arrays = layouts({k: np.asarray(v) for k, v in inputs.items()})
    aps = {k: nc.dram_tensor(k + "_dram", a.shape, _mybir.dt.from_np(a.dtype), kind="ExternalInput").ap() for k, a in arrays.items()}
    out = nc.dram_tensor("out_dram", arrays["x"].shape, _mybir.dt.float32, kind="ExternalOutput").ap()
    build(nc, aps, out, UPTO)
    r = _run(nc, [{k + "_dram": a for k, a in arrays.items()}], core_ids=[0])
    return r.results[0]["out_dram"]
```

```python
from contextlib import ExitStack

import numpy as np

import concourse.bass as bass
from concourse import mybir

ALU = mybir.AluOpType
ACT = mybir.ActivationFunctionType
AX = mybir.AxisListType
F32 = mybir.dt.float32
U32 = mybir.dt.uint32
F32R = mybir.dt.float32r

P = 128
BETA = 0.6
EPS = 1e-5
NSTATE = 16
NTAP = 4
QC = P - NSTATE
HEADS, HDIM = 16, 16
HROW = 32
EXPERTS = 8
SP_MAX = 40.0


class Sem:

    def __init__(self, nc, ctx, name):
        self.handle = ctx.enter_context(nc.semaphore(name))
        self.count = 0


class Queue:

    def __init__(self, nc, ctx, name, engine):
        self.engine, self.waited = engine, {}
        self.sem = Sem(nc, ctx, "done_" + name)

    def wait(self, *marks):
        for m in marks:
            if m is None or self.waited.get(m[0], 0) >= m[1]:
                continue
            self.waited[m[0]] = m[1]
            self.engine.wait_ge(m[0].handle, m[1])

    def do(self, f):
        f(self.engine)

    def mark(self, f):
        self.sem.count += 1
        f(self.engine).then_inc(self.sem.handle, 1)
        return (self.sem, self.sem.count)

    def load(self, sem, f):
        sem.count += 16
        f(self.engine).then_inc(sem.handle, 16)
        return (sem, sem.count)

    def last(self):
        return (self.sem, self.sem.count) if self.sem.count else None


def build(nc, d, out):
    B, S, D = d["x"].shape
    T = B * S
    NT, TB_, KD = T // P, S // P, D // P
    L = 2
    DI = d["w_dt"].shape[2]
    ET = DI // P
    RANK = 16
    NCH = -(-S // QC)
    CH = [min(QC, S - c * QC) for c in range(NCH)]
    WPAD = NCH * QC + NSTATE
    GN = 4
    F = d["up"].shape[3]
    FT = F // P

    with ExitStack() as ctx:
        pe, dve, act, pool, sp = (
            Queue(nc, ctx, n, e) for n, e in (("tensor", nc.tensor), ("vector", nc.vector), ("scalar", nc.scalar),
                                              ("gpsimd", nc.gpsimd), ("sync", nc.sync)))
        ALLQ = (pe, dve, act, pool, sp)

        def sb(c, name, shape, dt=F32):
            return c.enter_context(nc.sbuf_tensor(name, shape, dt))

        def sem(name):
            return Sem(nc, ctx, name)

        def load(name, dst, src, *after):
            sp.wait(*after)
            return sp.load(sem("ld_" + name), lambda e: e.dma_start(dst, src))

        def phase_border():
            marks = [q.last() for q in ALLQ]
            for q in ALLQ:
                q.wait(*marks)

        psum = ctx.enter_context(nc.psum_tensor("psum", [P, 8, 512], F32))

        ident = sb(ctx, "ident", [P, P])
        xm = sb(ctx, "xm", [P, NT, D])
        stat = sb(ctx, "stat", [P, NT, 12])
        epst = sb(ctx, "epst", [P, 1])
        xres = sb(ctx, "xres", [P, NT, D])
        w_early = sb(ctx, "w_early", [P, L * KD * 2 * DI])
        c_early = sb(ctx, "c_early", [P, NCH * DI])
        x_tok = d["x"].rearrange("b (t p) d -> p (b t) d", p=P)
        out_tok = out.rearrange("b (t p) d -> p (b t) d", p=P)

        ld_ident = load("ident", ident[:], d["ident"])
        ld_x = [load("x0", xm[:, 0:TB_, :], x_tok[:, 0:TB_, :])]
        m_eps = dve.mark(lambda e: e.memset(epst[:], EPS))

        def norm_pieces(lo, hi, src, src_marks):
            dve.wait(*src_marks)
            for t in range(lo, hi):
                m = dve.mark(lambda e, t=t: e.bn_stats(stat[:, t, 0:6], src[:, t, :]))
                if t % TB_ == TB_ - 1:
                    yield
            dve.wait(m)
            for t in range(lo, hi):
                m = dve.mark(lambda e, t=t: e.bn_aggr(stat[:, t, 6:8], stat[:, t, 0:6]))
            act.wait(m, m_eps)
            m = act.mark(lambda e: e.activation(stat[:, lo:hi, 8], stat[:, lo:hi, 7], ACT.Sqrt, bias=epst[:, 0:1]))
            yield
            dve.wait(m)
            m = dve.mark(lambda e: e.reciprocal(stat[:, lo:hi, 9], stat[:, lo:hi, 8]))
            dve.wait(m)
            for t in range(lo, hi):
                m = dve.mark(lambda e, t=t: e.tensor_scalar(xm[:, t, :], src[:, t, :], stat[:, t, 6:7], stat[:, t, 9:10],
                                                            ALU.subtract, ALU.mult))
                if t % TB_ == TB_ - 1 and t < hi - 1:
                    yield
            return m

        def at_once(g):
            while True:
                try:
                    next(g)
                except StopIteration as end:
                    return end.value

        def layernorm(b, src, src_marks):
            return at_once(norm_pieces(b * TB_, (b + 1) * TB_, src, src_marks))

        ATT_W = (("w_q", KD, P), ("w_k", KD, P), ("w_v", KD, 4 * P), ("w_o", HEADS // 4, D))

        def att_w(n):
            name, tiles, cols = ATT_W[n]
            q = w_early[:, n * 4 * D:(n + 1) * 4 * D]
            if cols == P:
                return q.rearrange("p (k g c) -> p k g c", k=tiles, c=cols)
            return q.rearrange("p (k c) -> p k c", k=tiles)

        ctxT = c_early[:, 0:2 * KD * S].rearrange("p (b k s) -> p b k s", b=2, k=KD)

        with ExitStack() as mc:
            assert L * KD * 2 * DI == 16 * D
            w_in = w_early[:].rearrange("p (l k f) -> p l k f", l=L, k=KD)
            w_xp = sb(mc, "w_xp", [P, L, ET, RANK + 2 * NSTATE])
            w_dt = sb(mc, "w_dt", [RANK, L, DI])
            w_out = sb(mc, "w_out", [P, L, ET, D])
            w_cv = sb(mc, "w_cv", [P, L, ET, NTAP])
            vecs = sb(mc, "vecs", [P, L, 3, ET])
            normw = sb(mc, "normw", [P, L, KD])
            alog = sb(mc, "alog", [P, L, ET, NSTATE])
            toep = sb(mc, "toep", [P, QC])
            keep = sb(mc, "keep", [P, 1])
            carry_id = sb(mc, "carry_id", [P, NCH, NSTATE])

            square = sb(mc, "square", [P, D])
            xnT = sb(mc, "xnT", [P, KD, S])
            xraw = sb(mc, "xraw", [P, ET, NTAP - 1 + S])
            xs = xraw[:, :, NTAP - 1:NTAP - 1 + D]
            uw = sb(mc, "uw", [P, ET, WPAD])
            xbs = sb(mc, "xbs", [P, 2, ET, WPAD])
            halves = xres[:].rearrange("p t d -> p (t d)").rearrange("p (h e s) -> p h e s", h=2, e=ET)
            delta = [halves[:, 0], sb(mc, "delta1", [P, ET, S])[:]]
            sz = [halves[:, 1], sb(mc, "sz1", [P, ET, S])[:]]
            RBC = RANK + 2 * NSTATE
            dbc = sb(mc, "dbc", [RBC, WPAD])
            uT = [c_early[:].rearrange("p (c e) -> p c e", c=NCH), sb(mc, "uT1", [P, NCH, DI])[:]]
            bcol = sb(mc, "bcol", [P, 2, NCH, NSTATE])
            bend = sb(mc, "bend", [P, NCH, NSTATE])
            ccol = sb(mc, "ccol", [P, 2, TB_, NSTATE])
            NG = NSTATE // GN
            filt = sb(mc, "filt", [P, 2, NCH, GN, QC])
            yacc = sb(mc, "yacc", [P, 2, TB_, DI])
            NDA, NH, AHEAD = 6, 9, 4
            dA = sb(mc, "dA", [P, NDA, S])
            hst = sb(mc, "hst", [P, NH, S])

            wt = {}
            wt["normw"] = load("normw", normw[:], d["normw"])
            wt["w_in", 0] = load("w_in0", w_in[:, 0], d["w_in"][:, 0])
            for name, dst in (("w_cv", w_cv), ("vecs", vecs), ("w_xp", w_xp),
                              ("w_dt", w_dt), ("alog", alog), ("toep", toep), ("keep", keep), ("carry_id", carry_id),
                              ("w_out", w_out)):
                wt[name] = load(name, dst[:], d[name])
            ld_x += [load(f"x{b}", xm[:, b * TB_:(b + 1) * TB_, :], x_tok[:, b * TB_:(b + 1) * TB_, :]) for b in range(1, B)]
            wt["w_in", 1] = load("w_in1", w_in[:, 1], d["w_in"][:, 1])

            m_zero = [pool.mark(lambda e: e.memset(xraw[:], 0.0)), pool.mark(lambda e: e.memset(uw[:], 0.0)),
                      pool.mark(lambda e: e.memset(xbs[:], 0.0)), pool.mark(lambda e: e.memset(dbc[:], 0.0))]
            v_free, t_free, x_free = [None] * 3, [None] * 3, [None] * 2
            cnt = {"v": 0, "t": 0, "x": 0, "a": 0, "h": 0}

            def bank(kind, base, free):
                i = cnt[kind] % len(free)
                cnt[kind] += 1
                pe.wait(free[i])
                return i, psum[:, base + i, :]

            def xbank():
                return bank("x", 6, x_free)

            def transpose4(dst, srcs):
                for j, s in enumerate(srcs):
                    f = lambda e, j=j, s=s: e.transpose(dst[:, j * P:(j + 1) * P], s, ident[:])
                    if j < len(srcs) - 1:
                        pe.do(f)
                return pe.mark(f)

            items = [(l, b) for l in range(L) for b in range(B)]
            n_items = len(items)
            stream = [None] * B
            rms = [None] * B

            sq_free = [None]

            def rms_squares(b):
                act.wait(stream[b], m_eps)
                for t in range(b * TB_, (b + 1) * TB_):
                    act.wait(sq_free[0])
                    sq_free[0] = act.mark(lambda e: e.activation(square[:], xm[:, t, :], ACT.Square, accum_out=stat[:, t, 10:11]))

            def rms_root(lo, hi):
                act.wait(sq_free[0])
                return act.mark(lambda e: e.activation(stat[:, lo * TB_:hi * TB_, 11], stat[:, lo * TB_:hi * TB_, 10], ACT.Sqrt,
                                                       scale=1.0 / D, bias=epst[:, 0:1]))

            def rms_inverse(lo, hi, m):
                dve.wait(m)
                m = dve.mark(lambda e: e.reciprocal(stat[:, lo * TB_:hi * TB_, 11], stat[:, lo * TB_:hi * TB_, 11]))
                rms[lo:hi] = [m] * (hi - lo)

            stream[0] = layernorm(0, xm, [ld_x[0]])
            rms_squares(0)
            rms_inverse(0, 1, rms_root(0, 1))

            def other_norms():
                m = yield from norm_pieces(TB_, NT, xm, ld_x[1:])
                stream[1:] = [m] * (B - 1)
                for b in range(1, B):
                    yield
                    rms_squares(b)
                m = rms_root(1, B)
                yield
                rms_inverse(1, B, m)
                yield

            act.wait(wt["alog"])
            m = act.mark(lambda e: e.activation(alog[:], alog[:], ACT.Exp))
            dve.wait(m)
            m_aneg = dve.mark(lambda e: e.tensor_scalar(alog[:], alog[:], -1.0, None, ALU.mult))

            done = [dict() for _ in range(n_items)]
            pe.wait(ld_ident)

            def front(k):
                l, b = items[k]
                par = k % 2
                me, old = done[k], done[k - 2] if k >= 2 else {}
                prev = done[k - 1] if k else {}
                t0 = b * TB_
                dve.wait(stream[b], rms[b], prev.get("xraw_read"), *m_zero)
                for t in range(TB_):
                    m = dve.mark(lambda e: e.tensor_scalar(xs[:, t, :], xm[:, t0 + t, :], stat[:, t0 + t, 11:12],
                                                           None, ALU.mult))
                yield
                pe.wait(m)
                for kt in range(KD):
                    i, bk = xbank()
                    me["xs_read"] = m = transpose4(bk, [xs[:, t, kt * P:(kt + 1) * P] for t in range(TB_)])
                    yield
                    dve.wait(m, prev.get("xnT_read"), wt["normw"])
                    x_free[i] = m_xn = dve.mark(lambda e: e.tensor_scalar(xnT[:, kt, :], bk, normw[:, l, kt:kt + 1],
                                                                          None, ALU.mult))
                yield

                def project(m8):
                    i, bk = xbank()
                    pe.wait(m_xn, wt["w_in", l])
                    for kt in range(KD):
                        f = lambda e: e.matmul(bk, w_in[:, l, kt, m8 * P:(m8 + 1) * P], xnT[:, kt, :],
                                               start=kt == 0, stop=kt == KD - 1)
                        m = pe.mark(f) if kt == KD - 1 else pe.do(f)
                    return i, bk, m

                for m4 in range(ET):
                    i, bk, m = project(m4)
                    yield
                    act.wait(m, me["xs_read"], *m_zero, prev.get("uw_read"), old.get("sz_read"), wt["w_cv"], wt["vecs"])
                    m_raw = act.mark(lambda e: e.copy(xraw[:, m4, NTAP - 1:], bk))
                    dst = uw[:, m4, NSTATE:NSTATE + S]
                    x_free[i] = m = act.mark(lambda e: e.activation(dst, bk, ACT.Identity, scale=w_cv[:, l, m4, NTAP - 1:NTAP],
                                                                       bias=vecs[:, l, 0, m4:m4 + 1]))
                    i, bk, m_z = project(ET + m4)
                    yield
                    for tap in range(NTAP - 1):
                        dve.wait(m)
                        m = dve.mark(lambda e: e.scalar_tensor_tensor(
                            out=dst, in0=xraw[:, m4, tap:tap + S], scalar=w_cv[:, l, m4, tap:tap + 1], in1=dst,
                            op0=ALU.mult, op1=ALU.add))
                    act.wait(m_z)
                    x_free[i] = act.mark(lambda e: e.copy(sz[par][:, m4, :], bk))
                me["conv"] = m
                me["xnT_read"] = pe.last()
                yield
                act.wait(m, old.get("xbs_read"), x_free[i])
                me["xbs"] = m = act.mark(lambda e: e.activation(xbs[:, par, :, NSTATE:NSTATE + S], uw[:, :, NSTATE:NSTATE + S], ACT.Silu))
                me["sz"] = act.mark(lambda e: e.activation(sz[par], sz[par], ACT.Silu))
                yield
                yield
                i, bk = xbank()
                pe.wait(m, wt["w_xp"])
                for kt in range(ET):
                    f = lambda e: e.matmul(bk[0:RBC, :], w_xp[:, l, kt, :], xbs[:, par, kt, NSTATE:NSTATE + S],
                                           start=kt == 0, stop=kt == ET - 1)
                    m = pe.mark(f) if kt == ET - 1 else pe.do(f)
                yield
                act.wait(m, prev.get("dbc_read"))
                x_free[i] = m_dbc = act.mark(lambda e: e.copy(dbc[:, NSTATE:NSTATE + S], bk[0:RBC, :]))
                yield
                i, bk = xbank()
                pe.wait(m_dbc)
                starts = [c * QC for c in range(NCH)] + [NSTATE + t * P for t in range(TB_)]
                for j, w0 in enumerate(starts):
                    f = lambda e: e.transpose(bk[:, j * RBC:(j + 1) * RBC], dbc[:, w0:w0 + P], ident[0:RBC, 0:RBC])
                    m = pe.mark(f) if j == len(starts) - 1 else pe.do(f)
                yield
                dve.wait(m, wt["keep"], wt["carry_id"], old.get("bcol_read"), old.get("ccol_read"))
                tv = bk[:, 0:len(starts) * RBC].rearrange("p (j r) -> p j r", r=RBC)
                m = dve.mark(lambda e: e.scalar_tensor_tensor(
                    out=bcol[:, par], in0=tv[:, 0:NCH, RANK:RANK + NSTATE], scalar=keep[:, 0:1], in1=carry_id[:],
                    op0=ALU.mult, op1=ALU.add))
                me["bcol"] = m
                x_free[i] = me["ccol"] = dve.mark(lambda e: e.tensor_copy(ccol[:, par], tv[:, NCH:, RANK + NSTATE:]))
                dve.wait(m, wt["toep"], prev.get("bend_read"))
                m_bend = dve.mark(lambda e: e.tensor_scalar(bend[:], bcol[:, par], toep[:, QC - 1:QC], None, ALU.mult))
                for m4 in range(ET):
                    i, bk = xbank()
                    pe.wait(m_dbc, wt["w_dt"])
                    m = pe.mark(lambda e: e.matmul(bk, w_dt[:, l, m4 * P:(m4 + 1) * P], dbc[0:RANK, NSTATE:NSTATE + S], start=True, stop=True))
                    yield
                    act.wait(m, old.get("delta_read"), me["conv"])
                    x_free[i] = m = act.mark(lambda e: e.activation(delta[par][:, m4, :], bk, ACT.Identity, bias=vecs[:, l, 1, m4:m4 + 1]))
                me["dbc_read"] = pe.last()
                yield
                dve.wait(m)
                m = dve.mark(lambda e: e.tensor_scalar(xraw[:, :, NTAP - 1:], delta[par], SP_MAX, None, ALU.min))
                yield
                xr = xraw[:, :, NTAP - 1:]
                act.wait(m)
                m2 = act.mark(lambda e: e.activation(xr, xr, ACT.Exp))
                if k + 1 < n_items and items[k + 1][0]:
                    rms_squares(items[k + 1][1])
                yield
                act.wait(m2)
                m2 = act.mark(lambda e: e.activation(xr, xr, ACT.Ln, bias=1.0))
                nb = items[k + 1][1] if k + 1 < n_items and items[k + 1][0] else None
                if nb is not None:
                    m_rms = rms_root(nb, nb + 1)
                yield
                yield
                yield
                if nb is not None:
                    rms_inverse(nb, nb + 1, m_rms)
                for m4 in range(ET):
                    dve.wait(m2)
                    m = dve.mark(lambda e: e.tensor_tensor(delta[par][:, m4, :], delta[par][:, m4, :], xraw[:, m4, NTAP - 1:], ALU.max))
                    pool.wait(m, me["xbs"], *m_zero)
                    m_u = pool.mark(lambda e: e.tensor_tensor(uw[:, m4, NSTATE:NSTATE + S], delta[par][:, m4, :],
                                                              xbs[:, par, m4, NSTATE:NSTATE + S], ALU.mult))
                    yield
                me["delta"] = me["xraw_read"] = m
                yield
                yield
                for c in range(NCH):
                    i, bk = xbank()
                    pe.wait(m_u)
                    m = transpose4(bk, [uw[:, et, c * QC:c * QC + P] for et in range(ET)])
                    yield
                    act.wait(m, old.get("uT_read"))
                    x_free[i] = m_uT = act.mark(lambda e: e.copy(uT[par][:, c, :], bk))
                me["uw_read"] = pe.last()
                for c in range(NCH - 1):
                    yield
                    i, bk = xbank()
                    pe.wait(m_bend, m_uT)
                    m = pe.mark(lambda e: e.matmul(bk[0:NSTATE, :], bend[:, c, :], uT[par][:, c, :], start=True, stop=True))
                    yield
                    act.wait(m, m_uT)
                    x_free[i] = m_uT = act.mark(lambda e: e.copy(uT[par][0:NSTATE, c + 1, :], bk[0:NSTATE, :]))
                me["bend_read"] = pe.last()
                me["uT"] = m_uT

            g_state = {"n": 0}
            filt_free = [None, None]

            def build_filter(k, g):
                slot = g_state["n"] % 2
                g_state["n"] += 1
                pool.wait(done[k]["bcol"], wt["toep"], filt_free[slot])
                par = k % 2
                m = pool.mark(lambda e: e.tensor_tensor(
                    filt[:, slot], toep[:, :].unsqueeze(1).unsqueeze(1).to_broadcast([P, NCH, GN, QC]),
                    bcol[:, par, :, g * GN:(g + 1) * GN].unsqueeze(3).to_broadcast([P, NCH, GN, QC]), ALU.mult))
                done[k]["bcol_read"] = m
                return slot, m

            dA_free, h_free = [None] * NDA, [None] * NH
            y_free = [None, None]
            ready_filter = {}

            def add_state(k, n, hs, t):
                par, me = k % 2, done[k]
                i, bk = bank("t", 3, t_free)
                pe.wait(hs[-1][1])
                m = transpose4(bk, [hst[:, s, t * P:(t + 1) * P] for s, _ in hs])
                c = ccol[:, par, t, n:n + 1]
                if n == 0:
                    dve.wait(m, y_free[par], me["ccol"])
                    f = lambda e: e.tensor_scalar(yacc[:, par, t, :], bk, c, None, ALU.mult)
                else:
                    dve.wait(m, me["y", t])
                    f = lambda e: e.scalar_tensor_tensor(out=yacc[:, par, t, :], in0=bk, scalar=c, in1=yacc[:, par, t, :],
                                                         op0=ALU.mult, op1=ALU.add)
                me["y", t] = t_free[i] = dve.mark(f)
                if t == TB_ - 1:
                    for s, _ in hs:
                        h_free[s] = pe.last()
                    if n == NSTATE - 1:
                        me["ccol_read"] = t_free[i]

            decayed = []

            def run_ahead():
                while len(decayed) <= AHEAD and cnt["a"] < n_items * NSTATE * ET:
                    k, n, et = cnt["a"] // (NSTATE * ET), cnt["a"] // ET % NSTATE, cnt["a"] % ET
                    me, l = done[k], items[k][0]
                    if "delta" not in me:
                        break
                    a = cnt["a"] % NDA
                    cnt["a"] += 1
                    act.wait(dA_free[a], me["delta"], m_aneg)
                    m = act.mark(lambda e: e.activation(dA[:, a, :], delta[k % 2][:, et, :], ACT.Exp, scale=alog[:, l, et, n:n + 1]))
                    decayed.append((a, m))
                    if (n, et) == (NSTATE - 1, ET - 1):
                        me["delta_read"] = m

            def main(k, pend, side):
                l, b = items[k]
                par = k % 2
                me = done[k]
                for n in range(NSTATE):
                    g = n // GN
                    slot, m_f = ready_filter[k, g]
                    if n % GN == 0 and g + 1 < NG:
                        ready_filter[k, g + 1] = build_filter(k, g + 1)
                    if g == NG - 1 and k + 1 < n_items and (k + 1, 0) not in ready_filter and "bcol" in done[k + 1]:
                        ready_filter[k + 1, 0] = build_filter(k + 1, 0)
                    hs = []
                    for et in range(ET):
                        i, bk = bank("v", 0, v_free)
                        pe.wait(m_f, me["uT"])
                        for c in range(NCH):
                            f = lambda e: e.matmul(bk[:, c * QC:c * QC + CH[c]], uT[par][:, c, et * P:(et + 1) * P],
                                                   filt[:, slot, c, n % GN, 0:CH[c]], start=True, stop=True)
                            m_v = pe.mark(f) if c == NCH - 1 else pe.do(f)
                        run_ahead()
                        a, m_a = decayed.pop(0)
                        s = cnt["h"] % NH
                        cnt["h"] += 1
                        dve.wait(m_v, m_a, h_free[s])
                        m_h = dve.mark(lambda e: e.tensor_tensor_scan(hst[:, s, :], dA[:, a, :], bk, 0.0, ALU.mult, ALU.add))
                        v_free[i] = dA_free[a] = m_h
                        hs.append((s, m_h))
                        if pend is not None:
                            add_state(*pend, et)
                        next(side, None)
                    if n % GN == GN - 1:
                        filt_free[slot] = pe.last()
                    pend = (k, n, hs)
                me["uT_read"] = pe.last()
                for _ in side:
                    pass
                if k + 1 < n_items and (k + 1, 0) not in ready_filter:
                    ready_filter[k + 1, 0] = build_filter(k + 1, 0)
                return pend

            def back(k):
                l, b = items[k]
                par = k % 2
                me = done[k]
                for et in range(ET):
                    i, bk = xbank()
                    pe.wait(*[me["y", t] for t in range(TB_)])
                    m = transpose4(bk, [yacc[:, par, t, et * P:(et + 1) * P] for t in range(TB_)])
                    yield
                    dve.wait(m, me["xbs"])
                    xd = xbs[:, par, et, NSTATE:NSTATE + S]
                    x_free[i] = m = dve.mark(lambda e: e.scalar_tensor_tensor(
                        out=xd, in0=xd, scalar=vecs[:, l, 2, et:et + 1], in1=bk, op0=ALU.mult, op1=ALU.add))
                    pool.wait(m, me["sz"])
                    m_g = pool.mark(lambda e: e.tensor_tensor(sz[par][:, et, :], sz[par][:, et, :], xd, ALU.mult))
                y_free[par] = pe.last()
                me["xbs_read"] = m_g
                yield
                yield
                for t in range(TB_):
                    i, bk = xbank()
                    pe.wait(m_g, wt["w_out"])
                    for kt in range(ET):
                        f = lambda e: e.matmul(bk[:, 0:D], sz[par][:, kt, t * P:(t + 1) * P], w_out[:, l, kt, :],
                                               start=kt == 0, stop=kt == ET - 1)
                        m = pe.mark(f) if kt == ET - 1 else pe.do(f)
                    yield
                    dve.wait(m)
                    x_free[i] = dve.mark(lambda e: e.tensor_tensor(xm[:, b * TB_ + t, :], xm[:, b * TB_ + t, :], bk[:, 0:D], ALU.add))
                me["sz_read"] = pe.last()
                stream[b] = dve.last()

            m_x1, early = [None] * B, {}

            def attention_inputs():
                last, even = done[n_items - 1], done[n_items - 2]
                for n, (name, _, _) in enumerate(ATT_W):
                    early[name] = load(name, att_w(n), d[name], last["xnT_read"])
                early["ctx"] = [load(f"ctx{b}", ctxT[:, b], d["ctxT"][b], even["uT_read"]) for b in range(2)]
                ld = [load(f"xres{b}", xres[:, b * TB_:(b + 1) * TB_, :], x_tok[:, b * TB_:(b + 1) * TB_, :],
                           even["delta_read"], even["sz_read"]) for b in range(B)]
                for b in range(B - 1):
                    yield
                    yield
                    add_x(b, ld[b])
                yield
                early["ln"] = yield from norm_pieces(0, TB_, xres, [m_x1[0]])
                early["x3"] = ld[B - 1]

            def add_x(b, ld):
                r = xres[:, b * TB_:(b + 1) * TB_, :]
                dve.wait(ld, stream[b])
                m_x1[b] = dve.mark(lambda e: e.tensor_tensor(r, r, xm[:, b * TB_:(b + 1) * TB_, :], ALU.add))

            def sides(k):
                for _ in range(ET):
                    yield
                if k:
                    yield from back(k - 1)
                else:
                    yield from other_norms()
                if k + 1 < n_items:
                    yield from front(k + 1)
                else:
                    yield from attention_inputs()

            at_once(front(0))
            ready_filter[0, 0] = build_filter(0, 0)
            pend = None
            for k in range(n_items):
                pend = main(k, pend, sides(k))
            for t in range(TB_):
                add_state(*pend, t)
            for _ in back(n_items - 1):
                pass
            add_x(B - 1, early["x3"])
        phase_border()

        raw0 = sb(ctx, "raw0", [P, 2, KD * F])
        parts0 = sb(ctx, "parts0", [P, 4 * KD * F], F32R)
        ld_raw0 = [load("up_first", raw0[:, 0].rearrange("p (k f) -> p k f", k=KD), d["up"][EXPERTS]),
                   load("down_first", raw0[:, 1].rearrange("p (k f) -> p k f", k=FT), d["down"][EXPERTS])]
        wh0, wl0 = (parts0[:, z * 2 * KD * F:(z + 1) * 2 * KD * F].rearrange("p (h c) -> p h c", h=2) for z in range(2))

        def split_weights(raw, wh, wl, *after):
            pool.wait(*after)
            for half in range(2):
                m = pool.mark(lambda e: e.tensor_copy(wh[:, half], raw[:, half]))
                pool.wait(m)
                m = pool.mark(lambda e: e.tensor_tensor(wl[:, half], raw[:, half], wh[:, half].bitcast(F32), ALU.subtract))
            return m

        with ExitStack() as ac:
            HG = HEADS // 4
            UH = HEADS // 2
            UG = UH // 4
            w_q, w_k, w_v, w_o = (att_w(n) for n in range(4))
            b_qk = sb(ac, "b_qk", [P, 2, HG])
            b_v = sb(ac, "b_v", [P, HEADS * HROW])
            b_o = sb(ac, "b_o", [P, D])
            xnT = sb(ac, "axnT", [P, KD, S])
            flat = sb(ac, "flat", [P, 2, S])
            part = parts0[:].rearrange("p (w h g t) -> p w h g t", w=2, h=2, g=UG)
            qk = sb(ac, "qk", [P, 2, 2, UH, S], F32R)
            vt = sb(ac, "vt", [P, 2, TB_, HEADS * HROW])
            nmax = sb(ac, "nmax", [P, 2, TB_, UH])
            nsplit = sb(ac, "nsplit", [P, 2, TB_, 2 * UH], F32R)
            nrow = sb(ac, "nrow", [2 * UH, 2, S], F32R)
            NPT = 2
            pT = sb(ac, "pT", [P, NPT, 4, S])
            oT = sb(ac, "oT", [P, HG, S])
            rc = sb(ac, "rc", [P, 4 * TB_])
            otok = sb(ac, "otok", [P, S])
            aw = {n: early[n] for n, _, _ in ATT_W}
            aw["b_qk"] = load("b_qk", b_qk[:], d["b_qk"])
            aw["b_v"] = load("b_v", b_v[:], d["b_v"].partition_broadcast(P))
            aw["b_o"] = load("b_o", b_o[:], d["b_o"].partition_broadcast(P))
            ld_ctx = early["ctx"]
            s_strip = [[sem(f"strips_{o}{i}") for i in range(2)] for o in ("sync", "gpsimd")]
            s_rows = [sem("rows0"), sem("rows1")]
            NPAIR, PV, ONE0, NONE = 2, 4, 5, 3
            pair_free, pv_free, one_free = [None] * NPAIR, [None], [None] * NONE
            pc = {"n": 0, "p": 0, "f": 0, "o": 0}
            pT_free, flat_free = [None] * NPT, [None, None]
            ctx_read, vt_read, oT_read, xnT_read, rc_read = [None, None], [None, None], [None], [None], [None]
            ud = [dict() for _ in range(2 * B)]
            m_ln = [None] * B
            m_v, m_x2, m_div = [None] * B, [None] * B, {}

            def one(f_list):
                i = pc["o"] % NONE
                pc["o"] += 1
                bk = psum[:, ONE0 + i, :]
                pe.wait(one_free[i])
                for f in f_list[:-1]:
                    pe.do(lambda e: f(e, bk))
                return i, bk, pe.mark(lambda e: f_list[-1](e, bk))

            def prepare(u):
                b, half = divmod(u, 2)
                cp, par, me = b % 2, u % 2, ud[u]
                prev, old = (ud[u - 1] if u else {}), (ud[u - 2] if u > 1 else {})
                if half == 0:
                    ln = layernorm(b, xres, [m_x1[b]]) if b else early["ln"]
                    yield
                    yield
                    for kt in range(KD):
                        pe.wait(ln)
                        i, bk, m = one([lambda e, bk, t=t: e.transpose(bk[:, t * P:(t + 1) * P], xm[:, b * TB_ + t, kt * P:(kt + 1) * P], ident[:])
                                 for t in range(TB_)])
                        yield
                        dve.wait(m, xnT_read[0])
                        one_free[i] = me["xn"] = dve.mark(lambda e: e.tensor_copy(xnT[:, kt, :], bk))
                else:
                    me["xn"] = prev["xn"]
                for g in range(UG):
                    for which, w, src, ready in ((1, w_k, ctxT[:, cp], ld_ctx[b]), (0, w_q, xnT, me["xn"])):
                        hg = half * UG + g
                        pe.wait(aw["w_k"], aw["w_q"], ready)
                        i, bk, m = one([lambda e, bk, kt=kt: e.matmul(bk, w[:, kt, hg, :], src[:, kt, :], start=kt == 0, stop=kt == KD - 1)
                                 for kt in range(KD)])
                        yield
                        z = pc["f"] % 2
                        pc["f"] += 1
                        act.wait(m, aw["b_qk"], flat_free[z])
                        one_free[i] = m = act.mark(lambda e: e.activation(flat[:, z, :], bk, ACT.Identity, bias=b_qk[:, which, hg:hg + 1]))
                        dve.wait(m, prev.get(("strips", 0)), prev.get(("strips", 1)))
                        hi, lo = part[:, which, 0, g, :], part[:, which, 1, g, :]
                        m = dve.mark(lambda e: e.tensor_copy(hi, flat[:, z, :]))
                        dve.wait(m)
                        flat_free[z] = m = dve.mark(lambda e: e.tensor_tensor(lo, flat[:, z, :], hi.bitcast(F32), ALU.subtract))
                if half:
                    xnT_read[0] = pe.last()
                me["parts"] = m
                yield
                if half == 0:
                    for kv in range(TB_):
                        pe.wait(aw["w_v"], ld_ctx[b])
                        i, bk, m = one([lambda e, bk, kt=kt: e.matmul(bk, ctxT[:, cp, kt, kv * P:(kv + 1) * P], w_v[:, kt, :],
                                                           start=kt == 0, stop=kt == KD - 1) for kt in range(KD)])
                        yield
                        dve.wait(m, aw["b_v"], vt_read[cp])
                        one_free[i] = m_v[b] = dve.mark(lambda e: e.tensor_tensor(vt[:, cp, kv, :], bk, b_v[:], ALU.add))
                else:
                    ctx_read[cp] = pe.last()
                    if b + 2 < B:
                        ld_ctx.append(load(f"ctx{b + 2}", ctxT[:, cp], d["ctxT"][b + 2], ctx_read[cp]))

            def strips(u):
                par, me = u % 2, ud[u]
                for queue in (sp, pool):
                    queue.wait(me["parts"], ud[u - 2]["qk_read"] if u > 1 else None)
                n = 0
                for strip, parts in enumerate(zip((0, 0, 1, 1), (0, 1, 0, 1))):
                    for which, p in enumerate(parts):
                        dst = qk[strip * HROW:(strip + 1) * HROW, par, which].rearrange("r (i g) t -> r i (g t)", i=4)
                        for i in range(4):
                            src = part[i * HROW:(i + 1) * HROW, which, p].rearrange("r g t -> r (g t)")
                            z = n % 8 in (1, 4, 6)
                            n += 1
                            m = (sp, pool)[z].load(s_strip[z][par], lambda e: e.dma_start(dst[:, i].bitcast(F32), src.bitcast(F32)))
                            me["strips", z] = m

            def pair(mms):
                i = pc["n"] % NPAIR
                pc["n"] += 1
                pe.wait(pair_free[i])
                pe.do(lambda e: mms[0](e, psum[:, 2 * i, :]))
                return i, pe.mark(lambda e: mms[1](e, psum[:, 2 * i + 1, :]))

            def maxima(u):
                par, me = u % 2, ud[u]
                old = ud[u - 2] if u > 1 else {}
                q, k = qk[:, par, 0], qk[:, par, 1]
                for h in range(0, UH, 2):
                    for t in range(TB_):
                        pe.wait(me["strips", 0], me["strips", 1])
                        i, m = pair([lambda e, o, h=h + j: e.matmul(o, q[:, h, t * P:(t + 1) * P], k[:, h, :], start=True, stop=True)
                                     for j in range(2)])
                        dve.wait(m, old.get("nmax_read"))
                        pair_free[i] = m = dve.mark(lambda e: e.tensor_reduce(nmax[:, par, t, h:h + 2], psum[:, 2 * i:2 * i + 2, :], AX.X,
                                                                              ALU.max, negate=True))
                        yield
                dve.wait(m, old.get("nsplit_read"))
                m = dve.mark(lambda e: e.tensor_copy(nsplit[:, par, :, 0:UH], nmax[:, par]))
                dve.wait(m)
                m = dve.mark(lambda e: e.tensor_tensor(nsplit[:, par, :, UH:], nmax[:, par], nsplit[:, par, :, 0:UH].bitcast(F32), ALU.subtract))
                me["nmax_read"] = m
                yield
                pe.wait(m, ld_ident)
                i, bk, m = one([lambda e, bk, t=t: e.transpose(bk[0:2 * UH, t * P:(t + 1) * P], nsplit[:, par, t, :].bitcast(F32), ident[:])
                         for t in range(TB_)])
                me["nsplit_read"] = m
                yield
                dve.wait(m, old.get("rows"))
                one_free[i] = m = dve.mark(lambda e: e.tensor_copy(nrow[:, par, :], bk[0:2 * UH, :]))
                sp.wait(m)
                for p in range(2):
                    r = 2 * p * HROW + HDIM
                    me["rows"] = sp.load(s_rows[par], lambda e: e.dma_start(qk[r:r + 1, par, 0, :, :].bitcast(F32),
                                                                     nrow[p * UH:(p + 1) * UH, par, :].bitcast(F32)))

            def weighted(u, side, row_side):
                b, half = divmod(u, 2)
                par, cp, me = u % 2, b % 2, ud[u]
                q, k = qk[:, par, 0], qk[:, par, 1]

                def values(g, kv, z, m_e):
                    hg = half * UG + g
                    pe.wait(m_e, m_v[b], pv_free[0])
                    for i in range(4):
                        c0 = (hg * 4 + i) * HROW
                        f = lambda e: e.matmul(psum[i * HROW:(i + 1) * HROW, PV, :], vt[:, cp, kv, c0:c0 + HROW], pT[:, z, i, :],
                                               start=kv == 0, stop=kv == TB_ - 1, tile_position=(0, i * HROW))
                        m = pe.mark(f) if i == 3 else pe.do(f)
                    pT_free[z] = m
                    if kv == TB_ - 1:
                        act.wait(m, oT_read[0])
                        pv_free[0] = m_div[hg] = act.mark(lambda e: e.copy(oT[:, hg, :], psum[:, PV, :]))

                def divide(g):
                    hg = half * UG + g
                    pe.wait(m_div[hg])
                    i, bk, m = one([lambda e, bk, t=t: e.transpose(bk[:, t * P:(t + 1) * P], oT[:, hg, t * P:(t + 1) * P], ident[:]) for t in range(TB_)])
                    yield
                    v = bk.rearrange("p (n r) -> p n r", r=HROW)
                    dve.wait(m)
                    m = dve.mark(lambda e: e.reciprocal(rc[:], v[:, :, HDIM]))
                    dve.wait(m, rc_read[0])
                    one_free[i] = m = dve.mark(lambda e: e.tensor_tensor(otok[:].rearrange("p (n r) -> p n r", r=HROW), v,
                                                                         rc[:].unsqueeze(2).to_broadcast([P, 4 * TB_, HROW]), ALU.mult))
                    yield
                    pe.wait(m)
                    i, bk, m = one([lambda e, bk, t=t: e.transpose(bk[:, t * P:(t + 1) * P], otok[:, t * P:(t + 1) * P], ident[:]) for t in range(TB_)])
                    rc_read[0] = m
                    yield
                    act.wait(m)
                    one_free[i] = m_div[hg] = act.mark(lambda e: e.copy(oT[:, hg, :], bk))

                before = None
                for g in range(UG):
                    for kv in range(TB_):
                        z = pc["p"] % NPT
                        pc["p"] += 1
                        for hp in range(2):
                            pe.wait(me["rows"])
                            i, m = pair([lambda e, o, h=(2 * hp + j) * UG + g: e.matmul(o, k[:, h, kv * P:(kv + 1) * P], q[:, h, :], start=True, stop=True)
                                         for j in range(2)])
                            act.wait(m, pT_free[z])
                            pair_free[i] = m_e = act.mark(lambda e: e.activation(pT[:, z, 2 * hp:2 * hp + 2], psum[:, 2 * i:2 * i + 2, :], ACT.Exp,
                                                                                 scale=HDIM ** -0.5))
                            slot = (g * TB_ + kv) * 2 + hp
                            for j in range(2 if slot < 8 else 3):
                                if slot >= ROWS_FROM and j < 2:
                                    next(row_side, None)
                                next(side, None)
                        if before is not None:
                            values(*before)
                            if before[1] == TB_ - 1:
                                rest.append(divide(before[0]))
                        before = (g, kv, z, m_e)
                me["qk_read"] = pe.last()
                values(*before)
                rest.append(divide(UG - 1))
                if half:
                    vt_read[cp] = pe.last()
                    rest.append(project_out(b))

            def project_out(b):
                for t in range(TB_):
                    if t:
                        yield
                    pe.wait(aw["w_o"], *m_div.values())
                    i, bk, m = one([lambda e, bk, hg=hg: e.matmul(bk[:, 0:D], oT[:, hg, t * P:(t + 1) * P], w_o[:, hg, :], start=hg == 0, stop=hg == HG - 1)
                             for hg in range(HG)])
                    dve.wait(m, aw["b_o"])
                    r = xres[:, b * TB_ + t, :]
                    one_free[i] = m = dve.mark(lambda e: e.tensor_tensor(r, r, bk[:, 0:D], ALU.add))
                    dve.wait(m)
                    m_x2[b] = dve.mark(lambda e: e.tensor_tensor(r, r, b_o[:], ALU.add))
                oT_read[0] = pe.last()
                yield
                m_ln[b] = yield from norm_pieces(b * TB_, (b + 1) * TB_, xres, [m_x2[b]])

            def alternate(*parts):
                parts = list(parts)
                while parts:
                    for g in list(parts):
                        if next(g, g) is g:
                            parts.remove(g)
                        else:
                            yield

            NU = 2 * B
            rest = []

            def leftovers():
                while rest:
                    yield from rest.pop(0)

            ROWS_FROM = 4

            def sides(u):
                yield from alternate(leftovers(), prepare(u + 2) if u + 2 < NU else iter(()))
                yield from leftovers()

            for _ in prepare(0):
                pass
            strips(0)
            for _ in prepare(1):
                pass
            strips(1)
            for _ in maxima(0):
                pass
            for u in range(NU):
                side, rows = sides(u), maxima(u + 1) if u + 1 < NU else iter(())
                weighted(u, side, rows)
                for _ in alternate(rows, side):
                    pass
                if u + 2 < NU:
                    strips(u + 2)
                elif u + 2 == NU:
                    m_w0 = split_weights(raw0, wh0, wl0, *ld_raw0, ud[u + 1]["strips", 0], ud[u + 1]["strips", 1])
            for _ in leftovers():
                pass
        phase_border()

        with ExitStack() as fc:
            w_g = sb(fc, "w_g", [P, KD, EXPERTS])
            raw = [raw0, sb(fc, "raw1", [P, 2, KD * F])]
            wh = [wh0, sb(fc, "wh1", [P, 2, KD * F], F32R)]
            wl = [wl0, sb(fc, "wl1", [P, 2, KD * F], F32R)]
            xn = sb(fc, "xn", [P, B, KD, S])
            xh = sb(fc, "xh", [P, B, KD, S], F32R)
            xl = sb(fc, "xl", [P, B, KD, S], F32R)
            NHB = 2
            h32 = sb(fc, "h32", [P, NHB, FT, S])
            hh = sb(fc, "hh", [P, NHB, FT, S], F32R)
            hl = sb(fc, "hl", [P, NHB, FT, S], F32R)
            gate = sb(fc, "gate", [P, NT, 48])
            gidx = sb(fc, "gidx", [P, NT, 8], U32)
            iota = sb(fc, "iota", [P, EXPERTS])
            order = [EXPERTS] + list(range(EXPERTS))
            raw_ld, raw_read, w_ready, w_read = {}, [None, None], {}, [None, None]

            def load_expert(j):
                x, z = order[j], j % 2
                raw_ld[j] = [load(f"up{x}", raw[z][:, 0].rearrange("p (k f) -> p k f", k=KD), d["up"][x], raw_read[z]),
                             load(f"down{x}", raw[z][:, 1].rearrange("p (k f) -> p k f", k=FT), d["down"][x], raw_read[z])]

            def split_expert(j):
                z = j % 2
                w_ready[j] = raw_read[z] = split_weights(raw[z], wh[z], wl[z], *raw_ld[j], w_read[z])

            ld_wg = load("w_g", w_g[:], d["w_g"])
            ld_iota = load("iota", iota[:], d["iota"])
            w_ready[0] = raw_read[0] = m_w0
            load_expert(1)

            hid_free, out_free = [None] * 4, [None] * 3
            c3 = {"h": 0, "o": 0, "t": 0}
            h_free = [None] * NHB
            m_x, m_cw = [None] * B, [None]
            m_res = [None] * NT

            def transpose_in(b):
                for kt in range(KD):
                    i = c3["t"] % 4
                    c3["t"] += 1
                    pe.wait(m_ln[b], hid_free[i])
                    for t in range(TB_):
                        f = lambda e: e.transpose(psum[:, i, t * P:(t + 1) * P], xm[:, b * TB_ + t, kt * P:(kt + 1) * P], ident[:])
                        m = pe.mark(f) if t == TB_ - 1 else pe.do(f)
                    act.wait(m)
                    hid_free[i] = m = act.mark(lambda e: e.copy(xn[:, b, kt, :], psum[:, i, :]))
                    dve.wait(m)
                    m = dve.mark(lambda e: e.tensor_copy(xh[:, b, kt, :], xn[:, b, kt, :]))
                    dve.wait(m)
                    m_x[b] = dve.mark(lambda e: e.tensor_tensor(xl[:, b, kt, :], xn[:, b, kt, :], xh[:, b, kt, :].bitcast(F32), ALU.subtract))

            def route():
                pe.wait(m_x[B - 1], ld_wg)
                for t in range(NT):
                    for kt in range(KD):
                        c0 = t % TB_ * P
                        f = lambda e: e.matmul(psum[:, 7, t * EXPERTS:(t + 1) * EXPERTS],
                                               xn[:, t // TB_, kt, c0:c0 + P], w_g[:, kt, :],
                                               start=kt == 0, stop=kt == KD - 1)
                        m = pe.mark(f) if (t, kt) == (NT - 1, KD - 1) else pe.do(f)
                yield
                lg = psum[:, 7, 0:NT * EXPERTS].rearrange("p (t x) -> p t x", x=EXPERTS)
                G = gate
                bc = lambda c: G[:, :, c:c + 1].to_broadcast([P, NT, EXPERTS])
                dve.wait(m, ld_iota)
                m = dve.mark(lambda e: e.tensor_reduce(G[:, :, 40], lg, AX.X, ALU.max))
                dve.wait(m)
                m = dve.mark(lambda e: e.tensor_tensor(G[:, :, 0:8], lg, bc(40), ALU.subtract))
                yield
                act.wait(m)
                m = act.mark(lambda e: e.activation(G[:, :, 0:8], G[:, :, 0:8], ACT.Exp))
                yield
                dve.wait(m)
                m = dve.mark(lambda e: e.tensor_reduce(G[:, :, 41], G[:, :, 0:8], AX.X, ALU.add))
                dve.wait(m)
                m = dve.mark(lambda e: e.reciprocal(G[:, :, 42], G[:, :, 41]))
                dve.wait(m)
                m = dve.mark(lambda e: e.tensor_tensor(G[:, :, 0:8], G[:, :, 0:8], bc(42), ALU.mult))
                dve.wait(m)
                yield
                for t in range(NT):
                    m = dve.mark(lambda e: e.max(gate[:, t, 8:16], gate[:, t, 0:8]))
                dve.wait(m)
                yield
                for t in range(NT):
                    m = dve.mark(lambda e: e.max_index(gidx[:, t, :], gate[:, t, 8:16], gate[:, t, 0:8]))
                m2 = dve.mark(lambda e: e.tensor_tensor(G[:, :, 43], G[:, :, 8], G[:, :, 9], ALU.add))
                dve.wait(m, m2)
                yield
                m = dve.mark(lambda e: e.reciprocal(G[:, :, 44], G[:, :, 43]))
                m2 = dve.mark(lambda e: e.tensor_copy(G[:, :, 46:48], gidx[:, :, 0:2]))
                dve.wait(m, m2)
                m = dve.mark(lambda e: e.tensor_tensor(G[:, :, 16:18], G[:, :, 8:10], G[:, :, 44:45].to_broadcast([P, NT, 2]), ALU.mult))
                dve.wait(m)
                for j in range(2):
                    yield
                    for t in range(NT):
                        m = dve.mark(lambda e: e.tensor_scalar(gate[:, t, 24 + 8 * j:32 + 8 * j], iota[:],
                                                               gate[:, t, 46 + j:47 + j], gate[:, t, 16 + j:17 + j],
                                                               ALU.is_equal, ALU.mult))
                dve.wait(m)
                m_cw[0] = dve.mark(lambda e: e.tensor_tensor(G[:, :, 24:32], G[:, :, 24:32], G[:, :, 32:40], ALU.add))

            def three(dst, ah, al, bh, bl, first, last):
                for n, (p, q) in enumerate(((ah, bh), (al, bh), (ah, bl))):
                    f = lambda e: e.matmul(dst, p, q, start=first and n == 0, stop=last and n == 2)
                    m = pe.mark(f) if last and n == 2 else pe.do(f)
                return m

            def hidden(j, b, hz):
                z = j % 2
                pe.wait(w_ready[j], m_x[b])
                for ft in range(FT):
                    i = c3["h"] % 4
                    c3["h"] += 1
                    pe.wait(hid_free[i])
                    for kt in range(KD):
                        w0 = kt * F + ft * P
                        m = three(psum[:, i, :], wh[z][:, 0, w0:w0 + P], wl[z][:, 0, w0:w0 + P], xh[:, b, kt, :], xl[:, b, kt, :],
                                  kt == 0, kt == KD - 1)
                    act.wait(m, h_free[hz])
                    hid_free[i] = m = act.mark(lambda e: e.activation(h32[:, hz, ft, :], psum[:, i, :], ACT.Gelu))
                    dve.wait(m, h_free[hz])
                    m = dve.mark(lambda e: e.tensor_copy(hh[:, hz, ft, :], h32[:, hz, ft, :]))
                    dve.wait(m)
                    m = dve.mark(lambda e: e.tensor_tensor(hl[:, hz, ft, :], h32[:, hz, ft, :], hh[:, hz, ft, :].bitcast(F32), ALU.subtract))
                    if (j, b) > (0, 0):
                        next(routing, None)
                return m

            def outputs(j, b, hz, m_h):
                x, z = order[j], j % 2
                pe.wait(m_h)
                for t in range(TB_):
                    i = c3["o"] % 3
                    c3["o"] += 1
                    pe.wait(out_free[i])
                    for ft in range(FT):
                        w0 = ft * D
                        m = three(psum[:, 4 + i, 0:D], hh[:, hz, ft, t * P:(t + 1) * P], hl[:, hz, ft, t * P:(t + 1) * P],
                                  wh[z][:, 1, w0:w0 + D], wl[z][:, 1, w0:w0 + D], ft == 0, ft == FT - 1)
                    tt = b * TB_ + t
                    r = xres[:, tt, :]
                    if x == EXPERTS:
                        dve.wait(m)
                        g = lambda e: e.tensor_tensor(r, r, psum[:, 4 + i, 0:D], ALU.add)
                    else:
                        dve.wait(m, m_res[tt], m_cw[0])
                        g = lambda e: e.scalar_tensor_tensor(out=r, in0=psum[:, 4 + i, 0:D], scalar=gate[:, tt, 24 + x:25 + x],
                                                             in1=r, op0=ALU.mult, op1=ALU.add)
                    m_res[tt] = out_free[i] = dve.mark(g)
                h_free[hz] = pe.last()

            stored = []
            for b in range(B):
                transpose_in(b)
            routing = route()
            steps = [(j, b) for j in range(len(order)) for b in range(B)]
            before = None
            for n, (j, b) in enumerate(steps):
                if b == 1 and j + 1 < len(order):
                    split_expert(j + 1)
                m_h = hidden(j, b, n % NHB)
                if b == 1 and j + 2 < len(order):
                    load_expert(j + 2)
                if before is not None:
                    outputs(*before)
                    if before[1] == B - 1:
                        w_read[before[0] % 2] = pe.last()
                before = (j, b, n % NHB, m_h)
            outputs(*before)

        s_out = sem("stored")
        for b in range(B):
            sp.wait(m_res[(b + 1) * TB_ - 1])
            m = sp.load(s_out, lambda e, b=b: e.dma_start(out_tok[:, b * TB_:(b + 1) * TB_, :], xres[:, b * TB_:(b + 1) * TB_, :]))
        sp.wait(m)


def shape_constants():
    f = np.float32
    toep = np.zeros((P, QC), np.float64)
    toep[:NSTATE] = BETA ** (np.arange(QC) + 1)
    for s in range(QC):
        toep[NSTATE + s, s:] = BETA ** np.arange(QC - s)
    keep = (np.arange(P) >= NSTATE).astype(f)[:, None]
    n_chunks = -(-512 // QC)
    carry_id = np.zeros((P, n_chunks, NSTATE), f)
    carry_id[:NSTATE] = np.eye(NSTATE, dtype=f)[:, None, :]
    return {"toep": toep.astype(f), "keep": keep, "carry_id": carry_id,
            "ident": np.eye(P, dtype=f), "iota": np.tile(np.arange(EXPERTS, dtype=f), (P, 1))}


def layouts(i):
    c = np.ascontiguousarray
    f = np.float32

    def tiles(a):
        *lead, k, n = a.shape
        return c(np.moveaxis(a.reshape(*lead, k // P, P, n), -2, 0))

    def cols(a):
        return c(a.reshape(a.shape[0], -1, P, a.shape[2]).transpose(2, 0, 1, 3))

    def strips(w):
        k = w.shape[0]
        o = np.zeros((k, HEADS, HROW), f)
        o[:, :, :HDIM] = w.reshape(k, HEADS, HDIM)
        return o.reshape(k, HEADS * HROW)

    d = dict(shape_constants())
    d["x"] = c(i["x"])
    d["w_in"] = tiles(i["L0_attn_in_proj_w"].transpose(0, 2, 1))
    d["w_xp"] = tiles(i["L0_attn_x_proj_w"].transpose(0, 2, 1))
    d["w_dt"] = c(i["L0_attn_dt_w"].transpose(2, 0, 1))
    d["w_out"] = tiles(i["L0_attn_out_w"].transpose(0, 2, 1))
    d["w_cv"] = cols(i["L0_attn_conv_w"])
    v = np.stack([i["L0_attn_conv_b"], i["L0_attn_dt_b"], i["L0_attn_Dp"]], 1)
    d["vecs"] = c(v.reshape(v.shape[0], 3, -1, P).transpose(3, 0, 1, 2))
    nw = i["L0_attn_norm_w"]
    d["normw"] = c(nw.reshape(nw.shape[0], -1, P).transpose(2, 0, 1))
    d["alog"] = cols(i["L0_attn_A_log"])
    ctx = i["ctx_1024"].transpose(0, 2, 1)
    d["ctxT"] = c(ctx.reshape(ctx.shape[0], -1, P, ctx.shape[2]).transpose(0, 2, 1, 3))
    for n, w in (("w_q", "Wq"), ("w_k", "Wk")):
        d[n] = c(tiles(strips(i["L0_xattn_" + w].T)).reshape(P, -1, HEADS // 4, P))
    d["w_v"] = tiles(strips(i["L0_xattn_Wv"].T))
    bq, bk, bv = (strips(i["L0_xattn_" + n][None])[0] for n in ("bq", "bk", "bv"))
    bk[HDIM::HROW] = 1
    bv[HDIM::HROW] = 1
    d["b_qk"] = c(np.stack([bq, bk]).reshape(2, -1, P).transpose(2, 0, 1))
    d["b_v"] = bv
    d["b_o"] = c(i["L0_xattn_bo"])
    d["w_o"] = tiles(strips(i["L0_xattn_Wo"]).T)
    d["w_g"] = tiles(i["L0_ffn_Wg"])
    d["up"] = c(np.moveaxis(tiles(np.concatenate([i["L0_ffn_Wu"], i["L0_ffn_W1"][None]])), 1, 0))
    d["down"] = c(np.moveaxis(tiles(np.concatenate([i["L0_ffn_Wd"], i["L0_ffn_W2"][None]])), 1, 0))
    return d


def kernel(**inputs):
    import concourse.bacc as _bacc
    from concourse import mybir as _mybir
    from concourse.bass_utils import run_bass_kernel_spmd as _run

    nc = _bacc.Bacc("TRN2", target_bir_lowering=False, num_devices=1)
    arrays = layouts({k: np.asarray(v) for k, v in inputs.items()})
    aps = {k: nc.dram_tensor(k + "_dram", a.shape, _mybir.dt.from_np(a.dtype), kind="ExternalInput").ap() for k, a in arrays.items()}
    out = nc.dram_tensor("out_dram", arrays["x"].shape, _mybir.dt.float32, kind="ExternalOutput").ap()
    build(nc, aps, out)
    r = _run(nc, [{k + "_dram": a for k, a in arrays.items()}], core_ids=[0])
    return r.results[0]["out_dram"]
```
